# Optimizing a Trainium2 kernel written in Bass

```python
import numpy as np
import jax
import jax.numpy as jnp

def _softmax(x, axis=-1):
    return jax.nn.softmax(x, axis=axis)

def _gelu(x):
    return jax.nn.gelu(x, approximate=True)

def _silu(x):
    return jax.nn.silu(x)

def _sigmoid(x):
    return jax.nn.sigmoid(x)

def _layernorm(x, axis=-1, eps=1e-05):
    m = jnp.mean(x, axis=axis, keepdims=True)
    v = jnp.var(x, axis=axis, keepdims=True)
    return (x - m) / jnp.sqrt(v + eps)

def _scatter_add(tgt, idx, src, axis=0):
    return tgt.at[idx].add(src)

def _segment_sum(src, seg, n):
    return jax.ops.segment_sum(src, seg, n)
kernel_name = 'mk_xattn_ffn_d1_seqx_r4_fb74bc'

def setup_inputs(seed: int=0):
    np.random.seed(seed)
    _w = jnp.asarray

    def _rec_inputs():
        import jax
        import jax.numpy as jnp
        _rk = jax.random.key(seed)
        x = -0.001547 + 1.001 * jax.random.normal(jax.random.fold_in(_rk, 1), (16, 112, 512), jnp.float32)
        _lenS = 112 - jax.random.randint(jax.random.fold_in(_rk, 7), (16,), 0, max(1, 112 // 4) + 1, jnp.int32)
        _lenS2 = 375 - jax.random.randint(jax.random.fold_in(_rk, 8), (16,), 0, max(1, 375 // 4) + 1, jnp.int32)
        _ctx_2048P = jax.random.normal(jax.random.fold_in(_rk, 12), (16, 16, 512), jnp.float32)
        _ctx_2048c = jax.random.dirichlet(jax.random.fold_in(_rk, 512), 0.3 * jnp.ones((16,), jnp.float32), (16, 375))
        _ctx_2048t = jnp.einsum('bsk,bkd->bsd', _ctx_2048c, _ctx_2048P)
        _ctx_2048t = _ctx_2048t * jax.lax.rsqrt(jnp.mean(jnp.square(_ctx_2048t)) + 1e-12) * 0.953939
        ctx_2048 = -5.72187e-05 + 0.999849 * (_ctx_2048t + 0.3 * jax.random.normal(jax.random.fold_in(_rk, 612), (16, 375, 512), jnp.float32))
        _validS = jnp.arange(112)[None, :] < _lenS[:, None]
        _validS2 = jnp.arange(375)[None, :] < _lenS2[:, None]
        _causal = jnp.tril(jnp.ones((112, 112), dtype=bool))
        mask_BxSxS2_ff0 = jnp.where(jnp.ones((16, 112, 375), dtype=bool), 0.0, -1000000000.0).astype(jnp.float32)
        return (x, ctx_2048, mask_BxSxS2_ff0)
    x, ctx_2048, mask_BxSxS2_ff0 = _rec_inputs()

    def _L0_xattn_setup():
        import jax, jax.numpy as jnp
        import numpy as np
        B, Q_LEN, E = (8, 16, 512)
        CACHE_LEN = 1024
        key = jax.random.key(seed)
        ks = jax.random.split(key, 9)
        s = 1.0 / np.sqrt(E)
        return {'x': jax.random.normal(ks[0], (B, Q_LEN, E), jnp.float32), 'attention_mask': jnp.zeros((B, Q_LEN, CACHE_LEN), jnp.float32), 'k_cache': jax.random.normal(ks[1], (B, CACHE_LEN, E), jnp.float32), 'v_cache': jax.random.normal(ks[2], (B, CACHE_LEN, E), jnp.float32), 'Wq': jax.random.normal(ks[3], (E, E), jnp.float32) * s, 'bq': jax.random.normal(ks[4], (E,), jnp.float32) * s, 'Wk': jax.random.normal(ks[5], (E, E), jnp.float32) * s, 'bk': jax.random.normal(ks[6], (E,), jnp.float32) * s, 'Wv': jax.random.normal(ks[7], (E, E), jnp.float32) * s, 'bv': jax.random.normal(ks[8], (E,), jnp.float32) * s}
    _L0_xattn_all = _L0_xattn_setup()
    _L0_xattn_in = {k: v for k, v in _L0_xattn_all.items() if k in ('Wq', 'bq', 'Wk', 'bk', 'Wv', 'bv')}
    del _L0_xattn_all

    def _L0_ffn_setup():
        import jax, jax.numpy as jnp
        import numpy as np
        BLOCK = 64

        def dequant4bit(q, scale):
            return (q.astype(jnp.float32) - 7.5) * jnp.repeat(scale, BLOCK, axis=1)
        key = jax.random.key(seed)
        ks = jax.random.split(key, 11)
        B, S, D, H, R = (4, 512, 512, 2048, 16)
        return {'x1': jax.random.normal(ks[0], (B, S, D), jnp.float32), 'w_up_q': jax.random.randint(ks[1], (H, D), 0, 16, dtype=jnp.int32), 'w_up_scale': jax.random.uniform(ks[2], (H, D // BLOCK), jnp.float32) * 0.02, 'b_up': jax.random.normal(ks[3], (H,), jnp.float32) * 0.01, 'w_up_lora_a': jax.random.normal(ks[4], (D, R), jnp.float32) * 0.02, 'w_up_lora_b': jax.random.normal(ks[5], (R, H), jnp.float32) * 0.02, 'w_down_q': jax.random.randint(ks[6], (D, H), 0, 16, dtype=jnp.int32), 'w_down_scale': jax.random.uniform(ks[7], (D, H // BLOCK), jnp.float32) * 0.02, 'b_down': jax.random.normal(ks[8], (D,), jnp.float32) * 0.01, 'w_down_lora_a': jax.random.normal(ks[9], (H, R), jnp.float32) * 0.02, 'w_down_lora_b': jax.random.normal(ks[10], (R, D), jnp.float32) * 0.02}
    _L0_ffn_all = _L0_ffn_setup()
    _L0_ffn_in = {k: v for k, v in _L0_ffn_all.items() if k in ('w_up_q', 'w_up_scale', 'b_up', 'w_up_lora_a', 'w_up_lora_b', 'w_down_q', 'w_down_scale', 'b_down', 'w_down_lora_a', 'w_down_lora_b')}
    del _L0_ffn_all
    return {'x': x, 'ctx_2048': ctx_2048, 'mask_BxSxS2_ff0': mask_BxSxS2_ff0, 'L0_xattn_Wq': _L0_xattn_in['Wq'], 'L0_xattn_bq': _L0_xattn_in['bq'], 'L0_xattn_Wk': _L0_xattn_in['Wk'], 'L0_xattn_bk': _L0_xattn_in['bk'], 'L0_xattn_Wv': _L0_xattn_in['Wv'], 'L0_xattn_bv': _L0_xattn_in['bv'], 'L0_ffn_w_up_q': _L0_ffn_in['w_up_q'], 'L0_ffn_w_up_scale': _L0_ffn_in['w_up_scale'], 'L0_ffn_b_up': _L0_ffn_in['b_up'], 'L0_ffn_w_up_lora_a': _L0_ffn_in['w_up_lora_a'], 'L0_ffn_w_up_lora_b': _L0_ffn_in['w_up_lora_b'], 'L0_ffn_w_down_q': _L0_ffn_in['w_down_q'], 'L0_ffn_w_down_scale': _L0_ffn_in['w_down_scale'], 'L0_ffn_b_down': _L0_ffn_in['b_down'], 'L0_ffn_w_down_lora_a': _L0_ffn_in['w_down_lora_a'], 'L0_ffn_w_down_lora_b': _L0_ffn_in['w_down_lora_b']}

def reference(x, ctx_2048, mask_BxSxS2_ff0, L0_xattn_Wq, L0_xattn_bq, L0_xattn_Wk, L0_xattn_bk, L0_xattn_Wv, L0_xattn_bv, L0_ffn_w_up_q, L0_ffn_w_up_scale, L0_ffn_b_up, L0_ffn_w_up_lora_a, L0_ffn_w_up_lora_b, L0_ffn_w_down_q, L0_ffn_w_down_scale, L0_ffn_b_down, L0_ffn_w_down_lora_a, L0_ffn_w_down_lora_b):
    import jax
    import jax.numpy as jnp

    def _L0_xattn_ref(x, attention_mask, k_cache, v_cache, Wq, bq, Wk, bk, Wv, bv):
        import jax, jax.numpy as jnp
        import numpy as np
        B, Q_LEN, E = (8, 16, 512)
        CACHE_LEN = 1024
        Q = jnp.einsum('bqe,fe->bqf', x, Wq) + bq
        K_new = jnp.einsum('bqe,fe->bqf', x, Wk) + bk
        V_new = jnp.einsum('bqe,fe->bqf', x, Wv) + bv
        q_len = x.shape[1]
        end_step = attention_mask.shape[-1]
        past_kv_len = end_step - q_len
        k_cache = jax.lax.dynamic_update_slice(k_cache, K_new, (0, past_kv_len, 0))
        v_cache = jax.lax.dynamic_update_slice(v_cache, V_new, (0, past_kv_len, 0))
        K = k_cache[:, :end_step, :]
        V = v_cache[:, :end_step, :]
        scale = 1.0 / jnp.sqrt(jnp.asarray(Q.shape[-1], Q.dtype))
        scores = jnp.einsum('bqe,bke->bqk', Q, K) * scale + attention_mask
        attn = jax.nn.softmax(scores, axis=-1)
        return jnp.einsum('bqk,bke->bqe', attn, V)

    def _L0_ffn_ref(x1, w_up_q, w_up_scale, b_up, w_up_lora_a, w_up_lora_b, w_down_q, w_down_scale, b_down, w_down_lora_a, w_down_lora_b):
        import jax, jax.numpy as jnp
        import numpy as np
        BLOCK = 64

        def dequant4bit(q, scale):
            return (q.astype(jnp.float32) - 7.5) * jnp.repeat(scale, BLOCK, axis=1)
        w_up = dequant4bit(w_up_q, w_up_scale).T
        y1 = x1 @ w_up + b_up + x1 @ w_up_lora_a @ w_up_lora_b
        x2 = jax.nn.relu(y1)
        w_down = dequant4bit(w_down_q, w_down_scale).T
        y2 = x2 @ w_down + b_down + x2 @ w_down_lora_a @ w_down_lora_b
        return y2
    x = x + _L0_xattn_ref(_layernorm(x, axis=-1), mask_BxSxS2_ff0, ctx_2048, ctx_2048, L0_xattn_Wq, L0_xattn_bq, L0_xattn_Wk, L0_xattn_bk, L0_xattn_Wv, L0_xattn_bv)
    x = x + _L0_ffn_ref(_layernorm(x, axis=-1), L0_ffn_w_up_q, L0_ffn_w_up_scale, L0_ffn_b_up, L0_ffn_w_up_lora_a, L0_ffn_w_up_lora_b, L0_ffn_w_down_q, L0_ffn_w_down_scale, L0_ffn_b_down, L0_ffn_w_down_lora_a, L0_ffn_w_down_lora_b)
    return x

_drawn_inputs = setup_inputs


def setup_inputs(seed=0):
    import zlib

    import numpy as np

    out = dict(_drawn_inputs(seed))
    spreads = {}
    factors = {'L0_xattn_bq': 7.641,
     'L0_xattn_bk': 8.0,
     'L0_xattn_bv': 4.114,
     'L0_ffn_b_up': 7.767,
     'L0_ffn_b_down': 8.0}
    for name, (base, spread) in spreads.items():
        noise = np.random.default_rng([zlib.crc32(name.encode()), seed]).standard_normal(out[name].shape)
        drawn = base * np.exp(spread * noise) if base else spread * noise
        out[name] = jnp.asarray(drawn.astype(out[name].dtype))
    for name, factor in factors.items():
        out[name] = (out[name] * factor).astype(out[name].dtype)
    return out
```

```python
from contextlib import ExitStack

import concourse.bass as bass
from concourse import mybir

ALU = mybir.AluOpType
ACT = mybir.ActivationFunctionType
F32 = mybir.dt.float32
F32R = mybir.dt.float32r
I32 = mybir.dt.int32

P = 128
B, S, E = 16, 112, 512
CTX = 263
KEYS = S + CTX
KPAD = KEYS + 1
VROWS = 3 * P - S
H, R = 2048, 16
KT_E = E // P
GB = 4
GS = GB * S
GROUPS = B // GB
HT = H // P
CHUNK = 512
TILES = B * S // P
CT = CHUNK // P
FULL = TILES // CT
REST = TILES - FULL * CT
EPS = 1e-5
SCALE = float(E) ** -0.5
ZERO_POINT = 7.5
PASSES = ((0, 0), (0, 1), (1, 0))


def build(nc, x, mask, ctx_k, ctx_v, w_qkv, b_qk, b_v, up_q, up_s, b_up, down_q, down_s, b_down,
          lora, y_mid, y_mid_rows, out):
    with ExitStack() as ctx:
        base = nc.sbuf_base

        class Map:
            def __init__(self, at):
                self.at = at

            def sb(self, name, shape, dt):
                size = 4
                for n in shape[1:]:
                    size *= n
                t = nc.alloc_sbuf_tensor_at(name, shape, dt, offset=self.at)
                self.at += (size + 31) // 32 * 32
                return t

        base = (base + 31) // 32 * 32
        m = Map(base)
        ident = m.sb("ident", [P, P], F32)
        bdown_row = m.sb("bdown_row", [P, E], F32)
        bqk_col = m.sb("bqk_col", [P, 2 * KT_E], F32)
        bq_scaled = m.sb("bq_scaled", [P, KT_E], F32)
        bup_col = m.sb("bup_col", [P, HT], F32)
        bn_raw = m.sb("bn_raw", [P, 2, 6], F32)
        mean_var = m.sb("mean_var", [P, 2, 2], F32)
        var_eps = m.sb("var_eps", [P, 2, 1], F32)
        minus_half = m.sb("minus_half", [P, 1], F32)
        gate = m.sb("gate", [P, 1], F32)
        rstd = m.sb("rstd", [P, 2, 1], F32)
        row_max = m.sb("row_max", [P, 2, 1], F32)
        minus_max = m.sb("minus_max", [P, 2, 1], F32)
        row_sum = m.sb("row_sum", [P, 2, 1], F32)
        inv_sum = m.sb("inv_sum", [P, 2, 1], F32)
        stage_at = m.at
        w_stage = m.sb("w_stage", [P, 3, KT_E * E], F32)
        phase_at = m.at
        m = Map(stage_at)
        lora_w = m.sb("lora_w", [P, 2 * (E + H)], F32R)
        y_res = Map(stage_at).sb("y_res", [P, CT, E], F32)
        m = Map(phase_at)
        bv_row = m.sb("bv_row", [P, E], F32)
        w_split = [m.sb(f"w_split{h}", [P, 3, KT_E, E], F32R) for h in range(2)]
        xT = [m.sb(f"xT{h}", [P, KT_E, GS], F32R) for h in range(2)]
        xT_next = m.sb("xT_next", [P, KT_E, GS], F32)
        qT = [m.sb(f"qT{h}", [P, KT_E, GS], F32R) for h in range(2)]
        k_raw = m.sb("k_raw", [P, GB, KT_E, KPAD], F32)
        kT = [m.sb(f"kT{h}", [P, KT_E, KPAD], F32R) for h in range(2)]
        lora_at = m.at
        v_raw = m.sb("v_raw", [P, 2, 3, E], F32)
        v_split = [m.sb(f"v_split{h}", [P, 3, E], F32R) for h in range(2)]
        mask_sb = m.sb("mask_sb", [P, 2, KEYS + 1], F32)
        logits = m.sb("logits", [P, 2, KEYS + 1], F32)
        probs = m.sb("probs", [P, 2, 3 * P], F32)
        pT = [m.sb(f"pT{h}", [P, 3, S], F32R) for h in range(2)]
        x_in = m.sb("x_in", [P, 2, E], F32)
        x_norm = m.sb("x_norm", [P, 2, E], F32)
        x_res = m.sb("x_res", [P, 2, E], F32)
        y_out = m.sb("y_out", [P, 2, E], F32)
        assert m.at <= nc.sbuf_usable_end, m.at
        lora_raw = Map(lora_at).sb("lora_raw", [P, 2 * (E + H)], F32)
        m = Map(phase_at)
        up_w = [m.sb(f"up_w{h}", [P, HT, KT_E, P], F32R) for h in range(2)]
        down_w = [m.sb(f"down_w{h}", [P, HT, E], F32R) for h in range(2)]
        zT = [m.sb(f"zT{h}", [P, KT_E, CHUNK], F32R) for h in range(2)]
        hid_raw = m.sb("hid_raw", [P, CHUNK], F32)
        hidT = [m.sb(f"hidT{h}", [P, 2, CHUNK], F32R) for h in range(2)]
        q_int = m.sb("q_int", [P, 2, 2, E], I32)
        w_real = m.sb("w_real", [P, 2, 2, E], F32)
        y_in = m.sb("y_in", [P, CT, E], F32)
        assert m.at <= nc.sbuf_usable_end, m.at

        ps = ctx.enter_context(nc.psum_tensor("ps", [P, 8, 512], F32))
        QK, LN_T, V_NEW, SCORES, P_T, AV = 0, 2, 3, 4, 5, 6
        ACC, HID, LORA_UP, LORA_DOWN, Z_T = 0, 4, 6, 7, 7

        def sem(name):
            return ctx.enter_context(nc.semaphore(name))

        s_x = [sem(f"s_x{n}") for n in range(2)]
        s_xres = [sem(f"s_xres{n}") for n in range(2)]
        s_kctx = [sem(f"s_kctx{n}") for n in range(GB)]
        s_vctx = [sem(f"s_vctx{n}") for n in range(2)]
        s_mask = [sem(f"s_mask{n}") for n in range(2)]
        s_w = [sem(f"s_w{n}") for n in range(3)]
        s_bias = sem("s_bias")
        s_lora_in = sem("s_lora_in")
        s_ymid = [sem(f"s_ymid{n}") for n in range(2)]
        s_y = [sem(f"s_y{n}") for n in range(CT)]
        s_res = [sem(f"s_res{n}") for n in range(CT)]
        s_q = [sem(f"s_q{n}") for n in range(2)]
        s_out = [sem(f"s_out{n}") for n in range(CT)]
        xt_t = sem("xt_t")
        kproj = sem("kproj")
        qproj = sem("qproj")
        vproj = sem("vproj")
        scored = sem("scored")
        p_t = sem("p_t")
        av_done = sem("av_done")
        z_t = sem("z_t")
        lora_up_done = sem("lora_up_done")
        lora_down_done = sem("lora_down_done")
        up_done = sem("up_done")
        down_done = sem("down_done")
        w_hi = sem("w_hi")
        lora_hi = sem("lora_hi")
        xt_evac = sem("xt_evac")
        xt_hi = sem("xt_hi")
        k_evac = sem("k_evac")
        q_hi = sem("q_hi")
        k_hi = sem("k_hi")
        v_hi = sem("v_hi")
        exp_done = sem("exp_done")
        p_hi = sem("p_hi")
        z_hi = sem("z_hi")
        up_hi = sem("up_hi")
        down_hi = sem("down_hi")
        hid_real = sem("hid_real")
        hid_hi = sem("hid_hi")
        w_lo = sem("w_lo")
        lora_lo = sem("lora_lo")
        bq_ready = sem("bq_ready")
        stats = sem("stats")
        stats_step = sem("stats_step")
        norm = sem("norm")
        xt_lo = sem("xt_lo")
        q_lo = sem("q_lo")
        k_lo = sem("k_lo")
        v_evac = sem("v_evac")
        v_lo = sem("v_lo")
        maxed = sem("maxed")
        soft = sem("soft")
        inv = sem("inv")
        p_lo = sem("p_lo")
        y_done = sem("y_done")
        z_lo = sem("z_lo")
        up_step = sem("up_step")
        down_step = sem("down_step")
        up_real = sem("up_real")
        down_real = sem("down_real")
        up_lo = sem("up_lo")
        down_lo = sem("down_lo")
        hid_lo = sem("hid_lo")
        out_done = sem("out_done")
        const_step = sem("const_step")
        const_ready = sem("const_ready")
        pads = sem("pads")
        root = sem("root")
        res_ready = sem("res_ready")

        block = ctx.enter_context(nc.Block())

        LAST = GROUPS - 1

        def groups(eng, body):
            body(0, True, False)
            with eng.Fori(1, LAST) as g:
                body(g, False, False)
            body(LAST, False, True)

        def chunks(eng, body):
            body(0, CT, CT, True)
            with eng.Fori(1, FULL - 1) as c:
                body(c, CT, CT, False)
            body(FULL - 1, CT, REST, False)
            body(FULL, REST, 0, False)

        UP_A, UP_B, DOWN_A, DOWN_B = 0, E, E + H, E + 2 * H

        @block.sync
        def _(sp):
            def load_x(b, slot):
                sp.dma_start(x_in[0:S, slot, :], x[b]).then_inc(s_x[slot], 16)

            def load_mask(b, slot):
                sp.dma_start(mask_sb[0:S, slot, 0:KEYS], mask[b]).then_inc(s_mask[slot], 16)

            def load_k(b, i):
                sp.dma_start(k_raw[:, i, :, S:KEYS], ctx_k[b]).then_inc(s_kctx[i], 16)

            def load_v(b, slot):
                sp.dma_start(v_raw[S:P, slot, 0, :], ctx_v[b, 0:P - S, :]).then_inc(s_vctx[slot], 16)
                sp.dma_start(v_raw[:, slot, 1:3, :],
                             ctx_v[b, P - S:VROWS, :].rearrange("(t p) e -> p t e", p=P)).then_inc(s_vctx[slot], 16)

            def load_res(b, slot):
                sp.dma_start(x_res[0:S, slot, :], x[b]).then_inc(s_xres[slot], 16)

            for b in range(2):
                load_x(b, b)
            sp.dma_start(w_stage[:, 1, :], w_qkv[1]).then_inc(s_w[1], 16)
            sp.dma_start(bqk_col[:], b_qk).then_inc(s_bias, 16)
            sp.dma_start(bup_col[:], b_up).then_inc(s_bias, 16)
            sp.dma_start(bv_row[:], b_v.partition_broadcast(P)).then_inc(s_bias, 16)
            sp.dma_start(bdown_row[:], b_down.partition_broadcast(P)).then_inc(s_bias, 16)
            sp.dma_start(w_stage[:, 0, :], w_qkv[0]).then_inc(s_w[0], 16)
            sp.dma_start(w_stage[:, 2, :], w_qkv[2]).then_inc(s_w[2], 16)
            for b in range(2, GB):
                sp.wait_ge(norm, b - 1)
                load_x(b, b % 2)
            for i in range(GB):
                load_k(i, i)
            sp.dma_start(lora_raw[:], lora).then_inc(s_lora_in, 16)
            for b in range(2):
                load_mask(b, b)
            load_res(0, 0)
            sp.wait_ge(lora_lo, 3)
            for b in range(2):
                load_v(b, b)

            def group(g, first, last):
                for i in range(GB):
                    b = g * GB + i
                    if not last:
                        sp.wait_ge(norm, b + 3)
                        load_x(b + GB, i % 2)
                    if not (first and i == 0):
                        sp.wait_ge(y_done, b)
                    if not (last and i == GB - 1):
                        load_res(b + 1, (i + 1) % 2)
                    if not (first and i == 0) and not (last and i == GB - 1):
                        sp.wait_ge(v_lo, b)
                        load_v(b + 1, (i + 1) % 2)
                    if not last:
                        sp.wait_ge(k_lo, b + 1)
                        load_k(b + GB, i)
                    if not (last and i >= GB - 2):
                        sp.wait_ge(maxed, b + 1)
                        load_mask(b + 2, i % 2)

            groups(sp, group)

            sp.wait_ge(y_done, B)
            for n in range(2):
                sp.wait_ge(s_ymid[n], 16 * (B // 2))

            def load_y(t, slot):
                sp.dma_start(y_in[:, slot, :], y_mid_rows[bass.ts(t, P), :]).then_inc(s_y[slot], 16)

            for j in range(CT):
                load_y(j, j)
            def next_rows(c, following):
                for j in range(following):
                    sp.wait_ge(z_t, c * CT + j + 1)
                    load_y(c * CT + CT + j, j)

            for n in range(HT):
                if n == 2:
                    next_rows(0, CT)
                k = n % 2
                if n >= 2:
                    sp.wait_ge(up_lo, n - 1)
                    sp.wait_ge(down_lo, n - 1)
                sp.dma_start(q_int[:, k, 0, :], up_q[n]).then_inc(s_q[k], 16)
                sp.dma_start(q_int[:, k, 1, :], down_q[n]).then_inc(s_q[k], 16)
                for half in range(2):
                    rows = slice(half * (P // 2), (half + 1) * (P // 2))
                    sp.dma_start(w_real[rows, k, 0, :], up_s[half, n].partition_broadcast(P // 2)).then_inc(s_q[k], 16)
                    sp.dma_start(w_real[rows, k, 1, :], down_s[half, n].partition_broadcast(P // 2)).then_inc(s_q[k], 16)

            def chunk(c, tiles, following, first):
                if not first:
                    next_rows(c, following)
                if first:
                    sp.wait_ge(lora_up_done, HT)
                    sp.wait_ge(lora_down_done, HT)
                for j in range(tiles):
                    if not first:
                        sp.wait_ge(s_out[j], 16 * c)
                    sp.dma_start(y_res[:, j, :], y_mid_rows[bass.ts(c * CT + j, P), :]).then_inc(s_res[j], 16)

            chunks(sp, chunk)
            for j in range(CT):
                sp.wait_ge(s_out[j], 16 * (FULL + (j < REST)))

        @block.gpsimd
        def _(pool):
            pool.memset(ident[:], 0.0).then_inc(const_step, 1)
            pool.memset(minus_half[:], -0.5).then_inc(const_step, 1)
            pool.wait_ge(const_step, 2)
            pool.affine_select(out=ident[:], in_=ident[:], compare_op=ALU.not_equal, fill=1.0, base=0,
                               pattern=[[-1, P]], channel_multiplier=1).then_inc(const_ready, 1)
            pool.memset(k_raw[:, :, :, KEYS:KPAD], 0.0).then_inc(pads, 1)
            pool.memset(probs[:, :, KEYS:3 * P], 0.0).then_inc(pads, 1)

            def inv_root(n, slot, rows):
                pool.wait_ge(stats, n + 1)
                pool.tensor_tensor(rstd[0:rows, slot, :], var_eps[0:rows, slot, :], minus_half[0:rows, :],
                                   ALU.pow).then_inc(root, 1)

            for b in range(GB):
                inv_root(b, b % 2, S)

            def store_mid(b, slot):
                pool.wait_ge(y_done, b + 1)
                pool.dma_start(y_mid[b], y_out[0:S, slot, :]).then_inc(s_ymid[slot], 16)

            def group(g, first, last):
                if not first:
                    store_mid(g * GB - 1, 1)
                for i in range(GB):
                    b = g * GB + i
                    if not last:
                        inv_root(b + GB, i % 2, S)
                    if i > 0:
                        store_mid(b - 1, (i - 1) % 2)

            groups(pool, group)
            store_mid(B - 1, 1)

            for j in range(CT):
                inv_root(B + j, j % 2, P)

            def chunk(c, tiles, following, first):
                for j in range(following):
                    inv_root(c * CT + (B + CT + j), j % 2, P)
                for j in range(tiles):
                    pool.wait_ge(s_res[j], 16 * c + 16)
                    pool.tensor_tensor(y_res[:, j, :], y_res[:, j, :], bdown_row[:], ALU.add).then_inc(res_ready, 1)
                for j in range(tiles):
                    pool.wait_ge(out_done, c * CT + j + 1)
                    pool.dma_start(out[bass.ts(c * CT + j, P), :], y_res[:, j, :]).then_inc(s_out[j], 16)

            chunks(pool, chunk)

        @block.scalar
        def _(act):
            def w_high(which):
                act.wait_ge(s_w[which], 16)
                act.activation(w_split[0][:, which, :, :].rearrange("p k f -> p (k f)"), w_stage[:, which, :],
                               ACT.Copy, scale=SCALE if which == 0 else 1.0).then_inc(w_hi, 1)

            def xt_evacuate(b, i):
                act.wait_ge(xt_t, b + 1)
                act.activation(xT_next[:, :, i * S:(i + 1) * S],
                               ps[:, LN_T, 0:KT_E * S].rearrange("p (k s) -> p k s", k=KT_E),
                               ACT.Copy).then_inc(xt_evac, 1)

            def v_high(b, half_b, slot):
                act.wait_ge(v_evac, b + 1)
                act.wait_ge(s_vctx[slot], half_b * 32 + 32)
                act.wait_ge(av_done, b)
                act.activation(v_split[0][:], v_raw[:, slot, :, :], ACT.Copy).then_inc(v_hi, 1)

            def v_high_first():
                act.wait_ge(v_evac, 1)
                act.wait_ge(s_vctx[0], 32)
                act.activation(v_split[0][:], v_raw[:, 0, :, :], ACT.Copy).then_inc(v_hi, 1)

            def p_high(b, first):
                act.wait_ge(p_t, b + 1)
                if not first:
                    act.wait_ge(av_done, b)
                act.activation(pT[0][:].rearrange("p t s -> p (t s)"), ps[:, P_T, 0:3 * S],
                               ACT.Copy).then_inc(p_hi, 1)

            def k_high(g, i, first):
                b = g * GB + i
                act.wait_ge(k_evac, g * KT_E + KT_E)
                act.wait_ge(s_kctx[i], 16 * g + 16)
                if first and i == 0:
                    act.wait_ge(pads, 2)
                else:
                    act.wait_ge(scored, b)
                act.activation(kT[0][:], k_raw[:, i, :, :], ACT.Copy).then_inc(k_hi, 1)

            w_high(1)
            for i in range(GB):
                xt_evacuate(i, i)

            def group(g, first, last):
                for k in range(KT_E):
                    if first and k == 0:
                        act.wait_ge(xt_evac, GB)
                    elif k == 0:
                        act.wait_ge(xt_evac, g * GB + GB)
                        act.wait_ge(vproj, g * GB)
                    act.activation(xT[0][:, k, :], xT_next[:, k, :], ACT.Copy).then_inc(xt_hi, 1)
                if first:
                    w_high(0)
                    w_high(2)
                    act.wait_ge(bq_ready, 1)
                    act.wait_ge(s_bias, 64)
                else:
                    v_high(g * GB - 1, g * 2 - 1, 1)
                    p_high(g * GB - 1, False)
                for f in range(KT_E):
                    n = g * KT_E + f
                    act.wait_ge(kproj, n + 1)
                    if not first:
                        act.wait_ge(k_lo, g * GB)
                    act.activation(k_raw[:, :, f, 0:S],
                                   ps[:, QK + f % 2, 0:GS].rearrange("p (b s) -> p b s", b=GB),
                                   ACT.Identity, bias=bqk_col[:, KT_E + f:KT_E + f + 1]).then_inc(k_evac, 1)
                k_high(g, 0, first)
                for f in range(KT_E):
                    act.wait_ge(qproj, g * KT_E + f + 1)
                    act.activation(qT[0][:, f, :], ps[:, QK + f % 2, 0:GS], ACT.Identity,
                                   bias=bq_scaled[:, f:f + 1]).then_inc(q_hi, 1)
                if first:
                    act.wait_ge(s_lora_in, 16)
                    act.wait_ge(w_lo, 3)
                    act.activation(lora_w[:], lora_raw[:], ACT.Copy).then_inc(lora_hi, 1)
                for i in range(GB):
                    b = g * GB + i
                    if i == 1 and first:
                        v_high_first()
                        p_high(0, True)
                    elif i > 0:
                        v_high(b - 1, g * 2 + (i - 1) // 2, (i - 1) % 2)
                        p_high(b - 1, False)
                    act.wait_ge(soft, b + 1)
                    if not (first and i < 2):
                        act.wait_ge(p_t, b - 1)
                        act.wait_ge(inv, b - 1)
                    act.activation(probs[0:S, i % 2, 0:KEYS], logits[0:S, i % 2, 0:KEYS], ACT.Exp,
                                   bias=minus_max[0:S, i % 2, :],
                                   accum_out=row_sum[0:S, i % 2, :]).then_inc(exp_done, 1)
                    if not last:
                        if i == 0:
                            act.wait_ge(xt_lo, g * KT_E + KT_E)
                        xt_evacuate(b + GB, i)
                    if i < GB - 1:
                        k_high(g, i + 1, first)

            groups(act, group)
            v_high(B - 1, B // 2 - 1, 1)
            p_high(B - 1, False)

            def z_high(t, j):
                act.wait_ge(z_t, t + 1)
                act.activation(zT[0][:, :, j * P:(j + 1) * P],
                               ps[:, Z_T - j % 2, :].rearrange("p (k s) -> p k s", k=KT_E),
                               ACT.Copy).then_inc(z_hi, 1)

            def hidden(c, n, width, first):
                act.wait_ge(up_done, c * HT + n + 1)
                if not (first and n == 0):
                    act.wait_ge(hid_lo, c * HT + n)
                act.activation(hid_raw[:, 0:width], ps[:, HID + n % 2, 0:width], ACT.Relu,
                               bias=bup_col[:, n:n + 1]).then_inc(hid_real, 1)
                if not (first and n < 2):
                    act.wait_ge(down_done, c * HT + n - 1)
                act.activation(hidT[0][:, n % 2, 0:width], ps[:, HID + n % 2, 0:width], ACT.Relu,
                               bias=bup_col[:, n:n + 1]).then_inc(hid_hi, 1)

            def up_high(n):
                act.wait_ge(up_real, n + 1)
                act.activation(up_w[0][:, n, :, :].rearrange("p k h -> p (k h)"), w_real[:, n % 2, 0, :],
                               ACT.Copy).then_inc(up_hi, 1)

            def down_high(n):
                act.wait_ge(down_real, n + 1)
                act.activation(down_w[0][:, n, :], w_real[:, n % 2, 1, :], ACT.Copy).then_inc(down_hi, 1)

            act.wait_ge(y_done, B)
            for j in range(CT):
                z_high(j, j)
            up_high(0)
            down_high(0)

            def chunk(c, tiles, following, first):
                for n in range(HT):
                    if first and n + 1 < HT:
                        up_high(n + 1)
                    hidden(c, n, tiles * P, first)
                    if first and n + 1 < HT:
                        down_high(n + 1)
                for j in range(following):
                    if j == 0:
                        act.wait_ge(up_done, c * HT + HT)
                    z_high(c * CT + CT + j, j)

            chunks(act, chunk)

        @block.vector
        def _(dve):
            def ln_stats(n, src, slot, rows):
                dve.bn_stats(bn_raw[0:rows, slot, :], src).then_inc(stats_step, 1)
                dve.wait_ge(stats_step, 2 * n + 1)
                dve.memset(gate[:], 0.0)
                dve.bn_aggr(mean_var[0:rows, slot, :], bn_raw[0:rows, slot, :]).then_inc(stats_step, 1)
                dve.wait_ge(stats_step, 2 * n + 2)
                dve.tensor_scalar(var_eps[0:rows, slot, :], mean_var[0:rows, slot, 1:2], EPS, None,
                                  ALU.add).then_inc(stats, 1)

            def ln_apply(n, dst, src, slot, rows):
                dve.wait_ge(root, n + 1)
                dve.tensor_scalar(dst, src, mean_var[0:rows, slot, 0:1], rstd[0:rows, slot, :],
                                  ALU.subtract, ALU.mult).then_inc(norm, 1)

            def x_stats(b, half_b, slot):
                dve.wait_ge(s_x[slot], half_b * 16 + 16)
                ln_stats(b, x_in[0:S, slot, :], slot, S)

            def x_apply(b, slot, fresh):
                if not fresh:
                    dve.wait_ge(xt_t, b - 1)
                ln_apply(b, x_norm[0:S, slot, :], x_in[0:S, slot, :], slot, S)

            def w_low(which, n):
                dve.wait_ge(w_hi, n + 1)
                hi = w_split[0][:, which, :, :].rearrange("p k f -> p (k f)").bitcast(F32)
                lo = w_split[1][:, which, :, :].rearrange("p k f -> p (k f)")
                dve.scalar_tensor_tensor(lo, w_stage[:, which, :], SCALE if which == 0 else 1.0, hi,
                                         ALU.mult, ALU.subtract).then_inc(w_lo, 1)

            for b in range(GB):
                x_stats(b, b // 2, b % 2)
                if b % 2:
                    x_apply(b - 1, 0, b < 2)
                    x_apply(b, 1, b < 2)
            w_low(1, 0)

            def v_evacuate(b, slot, fresh):
                dve.wait_ge(vproj, b + 1)
                if not fresh:
                    dve.wait_ge(v_lo, b - 1)
                dve.tensor_tensor(v_raw[0:S, slot, 0, :], ps[0:S, V_NEW, :], bv_row[0:S, :],
                                  ALU.add).then_inc(v_evac, 1)

            def v_low(b, slot):
                dve.wait_ge(v_hi, b + 1)
                dve.tensor_tensor(v_split[1][:], v_raw[:, slot, :, :], v_split[0][:].bitcast(F32),
                                  ALU.subtract).then_inc(v_lo, 1)

            def p_low(b):
                dve.wait_ge(p_hi, b + 1)
                dve.tensor_tensor(pT[1][:].rearrange("p t s -> p (t s)"), ps[:, P_T, 0:3 * S],
                                  pT[0][:].rearrange("p t s -> p (t s)").bitcast(F32),
                                  ALU.subtract).then_inc(p_lo, 1)

            def k_low(b, i):
                dve.wait_ge(k_hi, b + 1)
                dve.tensor_tensor(kT[1][:], k_raw[:, i, :, :], kT[0][:].bitcast(F32),
                                  ALU.subtract).then_inc(k_lo, 1)

            def softmax_shift(b, half_b, slot, fresh):
                dve.wait_ge(scored, b + 1)
                dve.wait_ge(s_mask[slot], half_b * 16 + 16)
                if not fresh:
                    dve.wait_ge(exp_done, b - 1)
                dve.memset(gate[:], 0.0)
                dve.tensor_tensor_reduce(logits[0:S, slot, 0:KEYS], ps[0:S, SCORES, 0:KEYS],
                                         mask_sb[0:S, slot, 0:KEYS], 1.0, -3.0e38, ALU.add, ALU.max,
                                         row_max[0:S, slot, :]).then_inc(maxed, 1)
                dve.wait_ge(maxed, b + 1)
                dve.tensor_scalar(minus_max[0:S, slot, :], row_max[0:S, slot, :], -1.0, None,
                                  ALU.mult).then_inc(soft, 1)

            def attended(b, half_b, slot, fresh):
                dve.wait_ge(exp_done, b + 1)
                dve.reciprocal(inv_sum[0:S, slot, :], row_sum[0:S, slot, :]).then_inc(inv, 1)
                dve.wait_ge(inv, b + 1)
                dve.wait_ge(av_done, b + 1)
                dve.wait_ge(s_xres[slot], half_b * 16 + 16)
                if not fresh:
                    dve.wait_ge(s_ymid[slot], half_b * 16)
                dve.scalar_tensor_tensor(y_out[0:S, slot, :], ps[0:S, AV, :], inv_sum[0:S, slot, :],
                                         x_res[0:S, slot, :], ALU.mult, ALU.add).then_inc(y_done, 1)

            def group(g, first, last):
                for k in range(KT_E):
                    dve.wait_ge(xt_hi, g * KT_E + k + 1)
                    dve.tensor_tensor(xT[1][:, k, :], xT_next[:, k, :], xT[0][:, k, :].bitcast(F32),
                                      ALU.subtract).then_inc(xt_lo, 1)
                if first:
                    w_low(0, 1)
                    w_low(2, 2)
                    dve.wait_ge(s_bias, 64)
                    dve.tensor_scalar(bq_scaled[:], bqk_col[:, 0:KT_E], SCALE, None, ALU.mult).then_inc(bq_ready, 1)
                else:
                    v_low(g * GB - 1, 1)
                    p_low(g * GB - 1)
                    attended(g * GB - 1, g * 2 - 1, 1, False)
                k_low(g * GB, 0)
                for f in range(KT_E):
                    n = g * KT_E + f
                    dve.wait_ge(q_hi, n + 1)
                    dve.scalar_tensor_tensor(qT[1][:, f, :], ps[:, QK + f % 2, 0:GS], bq_scaled[:, f:f + 1],
                                             qT[0][:, f, :].bitcast(F32), ALU.add, ALU.subtract).then_inc(q_lo, 1)
                if first:
                    dve.wait_ge(lora_hi, 1)
                    for at, rows, n in ((UP_A, slice(64, 128), E), (UP_B, slice(32, 64), H), (UP_B, slice(96, 128), H),
                                        (DOWN_A, slice(64, 128), H), (DOWN_B, slice(32, 64), E),
                                        (DOWN_B, slice(96, 128), E)):
                        part = lora_w[rows, at:at + n]
                        low = dve.tensor_tensor(part, lora_raw[rows, at:at + n], part.bitcast(F32), ALU.subtract)
                    low.then_inc(lora_lo, 3)
                for i in range(GB):
                    b = g * GB + i
                    if not last:
                        x_stats(b + GB, g * 2 + 2 + i // 2, i % 2)
                    if i > 0:
                        k_low(b, i)
                        v_low(b - 1, (i - 1) % 2)
                        p_low(b - 1)
                    if not last:
                        x_apply(b + GB, i % 2, False)
                    v_evacuate(b, i % 2, first and i < 2)
                    softmax_shift(b, g * 2 + i // 2, i % 2, first and i < 2)
                    if i > 0:
                        attended(b - 1, g * 2 + (i - 1) // 2, (i - 1) % 2, first and i < 3)

            groups(dve, group)
            v_low(B - 1, 1)
            p_low(B - 1)
            attended(B - 1, B // 2 - 1, 1, False)

            def y_stats(t, c16, slot, j):
                dve.wait_ge(s_y[j], c16)
                ln_stats(t + B, y_in[:, j, :], slot, P)

            def y_apply(t, slot, j):
                ln_apply(t + B, y_in[:, j, :], y_in[:, j, :], slot, P)

            def z_low(t, j):
                dve.wait_ge(z_hi, t + 1)
                dve.tensor_tensor(zT[1][:, :, j * P:(j + 1) * P],
                                  ps[:, Z_T - j % 2, :].rearrange("p (k s) -> p k s", k=KT_E),
                                  zT[0][:, :, j * P:(j + 1) * P].bitcast(F32), ALU.subtract).then_inc(z_lo, 1)

            def prepare(n):
                k = n % 2
                dve.wait_ge(s_q[k], 96 * (n // 2) + 96)
                for part, bank, step, real, product in ((0, LORA_UP, up_step, up_real, lora_up_done),
                                                        (1, LORA_DOWN, down_step, down_real, lora_down_done)):
                    w = w_real[:, k, part, :]
                    dve.scalar_tensor_tensor(w, q_int[:, k, part, :], -ZERO_POINT, w,
                                             ALU.add, ALU.mult).then_inc(step, 1)
                    dve.wait_ge(step, n + 1)
                    dve.wait_ge(product, n + 1)
                    dve.tensor_tensor(w, ps[:, bank, :], w, ALU.add).then_inc(real, 1)
                dve.wait_ge(up_hi, n + 1)
                dve.tensor_tensor(up_w[1][:, n, :, :].rearrange("p k h -> p (k h)"), w_real[:, k, 0, :],
                                  up_w[0][:, n, :, :].rearrange("p k h -> p (k h)").bitcast(F32),
                                  ALU.subtract).then_inc(up_lo, 1)
                dve.wait_ge(down_hi, n + 1)
                dve.tensor_tensor(down_w[1][:, n, :], w_real[:, k, 1, :], down_w[0][:, n, :].bitcast(F32),
                                  ALU.subtract).then_inc(down_lo, 1)

            for j in range(CT):
                y_stats(j, 16, j % 2, j)
                if j % 2:
                    y_apply(j - 1, 0, j - 1)
                    y_apply(j, 1, j)
            for j in range(CT):
                z_low(j, j)
            prepare(0)

            def chunk(c, tiles, following, first):
                for n in range(HT):
                    if first and n + 1 < HT:
                        prepare(n + 1)
                    if n % 2 == 0 and n >= HT // 2 and (n - HT // 2) // 2 < following:
                        j = (n - HT // 2) // 2
                        y_stats(c * CT + (CT + j), 16 * c + 32, j % 2, j)
                    dve.wait_ge(hid_hi, c * HT + n + 1)
                    if not (first and n < 2):
                        dve.wait_ge(down_done, c * HT + n - 1)
                    dve.tensor_tensor(hidT[1][:, n % 2, 0:tiles * P], hid_raw[:, 0:tiles * P],
                                      hidT[0][:, n % 2, 0:tiles * P].bitcast(F32), ALU.subtract).then_inc(hid_lo, 1)
                    if n % 2 == 0 and n >= HT // 2 and (n - HT // 2) // 2 < following:
                        j = (n - HT // 2) // 2
                        y_apply(c * CT + (CT + j), j % 2, j)
                for j in range(following):
                    z_low(c * CT + (CT + j), j)
                for j in range(tiles):
                    dve.wait_ge(down_done, c * HT + HT)
                    dve.wait_ge(res_ready, c * CT + j + 1)
                    dve.tensor_tensor(y_res[:, j, :], ps[:, ACC + j, :], y_res[:, j, :], ALU.add).then_inc(out_done, 1)

            chunks(dve, chunk)

        @block.tensor
        def _(pe):
            def product(dst, lhs, rhs, steps, done=None):
                n = len(PASSES) * steps
                for s in range(steps):
                    for a, b in PASSES:
                        i = s * len(PASSES) + PASSES.index((a, b))
                        last = pe.matmul(dst, lhs(a, s), rhs(b, s), start=(i == 0), stop=(i == n - 1))
                if done is not None:
                    last.then_inc(done, 1)

            def x_transpose(b, slot, fresh):
                pe.wait_ge(norm, b + 1)
                if not fresh:
                    pe.wait_ge(xt_evac, b)
                for k in range(KT_E):
                    last = pe.transpose(ps[:, LN_T, k * S:(k + 1) * S], x_norm[0:S, slot, k * P:(k + 1) * P],
                                        ident[0:S, 0:S])
                last.then_inc(xt_t, 1)

            def p_transpose(b, slot, fresh):
                pe.wait_ge(exp_done, b + 1)
                if fresh:
                    pe.wait_ge(pads, 2)
                else:
                    pe.wait_ge(p_lo, b)
                for t in range(3):
                    last = pe.transpose(ps[:, P_T, t * S:(t + 1) * S], probs[0:S, slot, t * P:(t + 1) * P],
                                        ident[0:S, 0:S])
                last.then_inc(p_t, 1)

            def attend(b, fresh):
                pe.wait_ge(p_lo, b + 1)
                pe.wait_ge(v_lo, b + 1)
                if not fresh:
                    pe.wait_ge(y_done, b)
                product(ps[0:S, AV, :], lambda h, t: pT[h][:, t, :], lambda h, t: v_split[h][:, t, :], 3, av_done)

            pe.wait_ge(const_ready, 1)
            for b in range(GB):
                x_transpose(b, b % 2, b == 0)

            def group(g, first, last):
                if not first:
                    p_transpose(g * GB - 1, 1, False)
                for which, done in ((1, kproj), (0, qproj)):
                    if first:
                        pe.wait_ge(w_lo, 2 - which)
                    for f in range(KT_E):
                        if which == 1 and f < 2 and not first:
                            pe.wait_ge(q_lo, g * KT_E - 1 + f)
                        elif which == 1 and f >= 2:
                            pe.wait_ge(k_evac, g * KT_E + f - 1)
                        elif which == 0 and f < 2:
                            pe.wait_ge(k_evac, g * KT_E + f + 3)
                        elif which == 0:
                            pe.wait_ge(q_lo, g * KT_E + f - 1)
                        for k in range(KT_E):
                            if which == 1 and f == 0:
                                pe.wait_ge(xt_lo, g * KT_E + k + 1)
                            for a, b in PASSES:
                                mm = pe.matmul(ps[:, QK + f % 2, 0:GS],
                                               w_split[a][:, which, k, f * P:(f + 1) * P], xT[b][:, k, :],
                                               start=(k == 0 and (a, b) == PASSES[0]),
                                               stop=(k == KT_E - 1 and (a, b) == PASSES[-1]))
                        mm.then_inc(done, 1)
                    if which == 1 and not first:
                        attend(g * GB - 1, False)
                if first:
                    pe.wait_ge(w_lo, 3)
                for i in range(GB):
                    b = g * GB + i
                    if i > 0:
                        p_transpose(b - 1, (i - 1) % 2, first and i == 1)
                    if not (first and i == 0):
                        pe.wait_ge(v_evac, b)
                    product(ps[0:S, V_NEW, :], lambda h, k: xT[h][:, k, i * S:(i + 1) * S],
                            lambda h, k: w_split[h][:, 2, k, :], KT_E, vproj)
                    if not last:
                        x_transpose(b + GB, i % 2, False)
                    pe.wait_ge(k_lo, b + 1)
                    pe.wait_ge(q_lo, g * KT_E + KT_E)
                    if not (first and i == 0):
                        pe.wait_ge(maxed, b)
                    product(ps[0:S, SCORES, 0:KPAD], lambda h, k: qT[h][:, k, i * S:(i + 1) * S],
                            lambda h, k: kT[h][:, k, :], KT_E, scored)
                    if i > 0:
                        attend(b - 1, first and i == 1)

            groups(pe, group)
            p_transpose(B - 1, 1, False)
            attend(B - 1, False)

            def z_transpose(t, j, fresh):
                pe.wait_ge(norm, t + B + 1)
                if not fresh:
                    pe.wait_ge(z_lo, t - 1)
                for k in range(KT_E):
                    last = pe.transpose(ps[:, Z_T - j % 2, k * P:(k + 1) * P], y_in[:, j, k * P:(k + 1) * P], ident[:])
                last.then_inc(z_t, 1)

            def lora_products(n):
                if n > 0:
                    pe.wait_ge(up_real, n)
                for k in range(KT_E):
                    last = pe.matmul(ps[:, LORA_UP, k * P:(k + 1) * P], lora_w[:, UP_A + k * P:UP_A + (k + 1) * P],
                                     lora_w[:, UP_B + n * P:UP_B + (n + 1) * P], start=True, stop=True)
                last.then_inc(lora_up_done, 1)
                if n > 0:
                    pe.wait_ge(down_real, n)
                pe.matmul(ps[:, LORA_DOWN, :], lora_w[:, DOWN_A + n * P:DOWN_A + (n + 1) * P],
                          lora_w[:, DOWN_B:DOWN_B + E], start=True, stop=True).then_inc(lora_down_done, 1)

            def up(c, n, width, first):
                if first:
                    pe.wait_ge(up_lo, n + 1)
                if not (first and n < 2):
                    pe.wait_ge(hid_hi, c * HT + n - 1)
                product(ps[:, HID + n % 2, 0:width], lambda h, k: up_w[h][:, n, k, :],
                        lambda h, k: zT[h][:, k, 0:width], KT_E, up_done)

            def down(c, n, tiles, first):
                if first:
                    pe.wait_ge(down_lo, n + 1)
                pe.wait_ge(hid_lo, c * HT + n + 1)
                for j in range(tiles):
                    if n == 0 and not first:
                        pe.wait_ge(out_done, (c - 1) * CT + j + 1)
                    for a, b in PASSES:
                        mm = pe.matmul(ps[:, ACC + j, :], hidT[a][:, n % 2, j * P:(j + 1) * P], down_w[b][:, n, :],
                                       start=(n == 0 and (a, b) == PASSES[0]),
                                       stop=(n == HT - 1 and (a, b) == PASSES[-1]))
                mm.then_inc(down_done, 1)


            for j in range(CT):
                z_transpose(j, j, j < 2)
            for j in range(2):
                pe.wait_ge(z_lo, CT - 1 + j)
            lora_products(0)

            def chunk(c, tiles, following, first):
                for n in range(HT):
                    if first and n + 1 < HT:
                        lora_products(n + 1)
                    if n == 0:
                        pe.wait_ge(z_lo, c * CT + tiles)
                    up(c, n, tiles * P, first)
                    if n > 0:
                        down(c, n - 1, tiles, first)
                if first:
                    pe.wait_ge(up_real, HT)
                    pe.wait_ge(down_real, HT)
                for j in range(min(2, following)):
                    z_transpose(c * CT + (CT + j), j, False)
                down(c, HT - 1, tiles, first)
                for j in range(2, following):
                    z_transpose(c * CT + (CT + j), j, False)

            chunks(pe, chunk)


def kernel(x, ctx_2048, mask_BxSxS2_ff0, L0_xattn_Wq, L0_xattn_bq, L0_xattn_Wk, L0_xattn_bk, L0_xattn_Wv,
           L0_xattn_bv, L0_ffn_w_up_q, L0_ffn_w_up_scale, L0_ffn_b_up, L0_ffn_w_up_lora_a, L0_ffn_w_up_lora_b,
           L0_ffn_w_down_q, L0_ffn_w_down_scale, L0_ffn_b_down, L0_ffn_w_down_lora_a, L0_ffn_w_down_lora_b):
    import concourse.bacc as bacc
    import numpy as np
    from concourse.bass_utils import run_bass_kernel_spmd

    x, ctx, mask = (np.asarray(a) for a in (x, ctx_2048, mask_BxSxS2_ff0))
    tail = ctx[:, :CTX]
    mask = np.concatenate([mask[:, :, CTX:], mask[:, :, :CTX]], axis=2)
    ctx_k = tail.reshape(B, CTX, KT_E, P).transpose(0, 3, 2, 1)
    ctx_v = np.zeros((B, VROWS, E), ctx.dtype)
    ctx_v[:, :CTX] = tail
    w_qkv = np.stack([np.asarray(w).reshape(E, KT_E, P).transpose(2, 1, 0).reshape(P, KT_E * E)
                      for w in (L0_xattn_Wq, L0_xattn_Wk, L0_xattn_Wv)])
    b_qk = np.concatenate([np.asarray(b).reshape(KT_E, P).T for b in (L0_xattn_bq, L0_xattn_bk)], axis=1)
    per = P // 64
    up_q = np.asarray(L0_ffn_w_up_q).reshape(HT, P, KT_E, P).transpose(0, 3, 2, 1).reshape(HT, P, E)
    up_s = np.asarray(L0_ffn_w_up_scale).reshape(HT, P, KT_E, per).transpose(3, 0, 2, 1).reshape(per, HT, E)
    down_q = np.asarray(L0_ffn_w_down_q).reshape(E, HT, P).transpose(1, 2, 0)
    down_s = np.asarray(L0_ffn_w_down_scale).reshape(E, HT, per).transpose(2, 1, 0)
    factors = np.concatenate([np.asarray(L0_ffn_w_up_lora_a).T, np.asarray(L0_ffn_w_up_lora_b),
                              np.asarray(L0_ffn_w_down_lora_a).T, np.asarray(L0_ffn_w_down_lora_b)], axis=1)
    lora = np.zeros((P, 2 * (E + H)), factors.dtype)
    for quadrant in range(4):
        lora[quadrant * 32:quadrant * 32 + R] = factors
    arrays = {
        "x": x, "mask": mask, "ctx_k": ctx_k, "ctx_v": ctx_v, "w_qkv": w_qkv, "b_qk": b_qk,
        "b_v": np.asarray(L0_xattn_bv), "up_q": up_q, "up_s": up_s,
        "b_up": np.asarray(L0_ffn_b_up).reshape(HT, P).T, "down_q": down_q, "down_s": down_s,
        "b_down": np.asarray(L0_ffn_b_down), "lora": lora,
    }
    arrays = {f"in_{name}": np.ascontiguousarray(a) for name, a in arrays.items()}
    nc = bacc.Bacc("TRN2", target_bir_lowering=False, num_devices=1)
    args = {name[3:]: nc.dram_tensor(name, a.shape, mybir.dt.from_np(a.dtype), kind="ExternalInput").ap()
            for name, a in arrays.items()}
    y_mid = nc.dram_tensor("y_mid", (B, S, E), F32, kind="Internal").ap()
    out = nc.dram_tensor("out_0", (B * S, E), F32, kind="ExternalOutput").ap()
    build(nc, y_mid=y_mid, y_mid_rows=y_mid.rearrange("b s e -> (b s) e"), out=out, **args)
    result = run_bass_kernel_spmd(nc, [arrays], core_ids=[0])
    return result.results[0]["out_0"].reshape(B, S, E)
```

```python
from contextlib import ExitStack

import concourse.bass as bass
from concourse import mybir

ALU = mybir.AluOpType
ACT = mybir.ActivationFunctionType
F32 = mybir.dt.float32
F32R = mybir.dt.float32r
I32 = mybir.dt.int32

P = 128
B, S, E = 16, 112, 512
CTX = 263
KEYS = S + CTX
KPAD = KEYS + 1
VROWS = 3 * P - S
H, R = 2048, 16
KT_E = E // P
GB = 4
GS = GB * S
GROUPS = B // GB
HT = H // P
CHUNK = 512
TILES = B * S // P
CT = CHUNK // P
FULL = TILES // CT
REST = TILES - FULL * CT
EPS = 1e-5
SCALE = float(E) ** -0.5
ZERO_POINT = 7.5
EARLY = 2
PASSES = ((0, 0), (0, 1), (1, 0))


def build(nc, x, mask, ctx_k, ctx_v, w_qkv, b_qk, b_v, up_q, up_s, b_up, down_q, down_s, b_down,
          lora, y_mid, y_mid_rows, out):
    with ExitStack() as ctx:
        base = nc.sbuf_base

        class Map:
            def __init__(self, at):
                self.at = at

            def sb(self, name, shape, dt):
                size = 4
                for n in shape[1:]:
                    size *= n
                t = nc.alloc_sbuf_tensor_at(name, shape, dt, offset=self.at)
                self.at += (size + 31) // 32 * 32
                return t

        base = (base + 31) // 32 * 32
        m = Map(base)
        ident = m.sb("ident", [P, P], F32)
        bdown_row = m.sb("bdown_row", [P, E], F32)
        bqk_col = m.sb("bqk_col", [P, 2 * KT_E], F32)
        bq_scaled = m.sb("bq_scaled", [P, KT_E], F32)
        bup_col = m.sb("bup_col", [P, HT], F32)
        bn_raw = m.sb("bn_raw", [P, 2, 6], F32)
        mean_var = m.sb("mean_var", [P, 2, 2], F32)
        var_eps = m.sb("var_eps", [P, 2, 1], F32)
        minus_half = m.sb("minus_half", [P, 1], F32)
        gate = m.sb("gate", [P, 1], F32)
        rstd = m.sb("rstd", [P, 2, 1], F32)
        row_max = m.sb("row_max", [P, 2, 1], F32)
        minus_max = m.sb("minus_max", [P, 2, 1], F32)
        row_sum = m.sb("row_sum", [P, 2, 1], F32)
        inv_sum = m.sb("inv_sum", [P, 2, 1], F32)
        stage_at = m.at
        w_stage = m.sb("w_stage", [P, 3, KT_E * E], F32)
        phase_at = m.at
        m = Map(stage_at)
        lora_w = m.sb("lora_w", [P, 2 * (E + H)], F32R)
        y_res = Map(stage_at).sb("y_res", [P, CT, E], F32)
        m = Map(phase_at)
        qk_split = [m.sb(f"qk_split{h}", [P, 2, KT_E, E], F32R) for h in range(2)]
        rows_at = m.at
        xT = [m.sb(f"xT{h}", [P, KT_E, GS], F32R) for h in range(2)]
        xT_next = m.sb("xT_next", [P, KT_E, GS], F32)
        x_in = m.sb("x_in", [P, GB, E], F32)
        rest_at = m.at
        bv_row = m.sb("bv_row", [P, E], F32)
        k_raw = m.sb("k_raw", [P, GB, KT_E, KPAD], F32)
        wv_split = [m.sb(f"wv_split{h}", [P, KT_E, E], F32R) for h in range(2)]
        qT = [m.sb(f"qT{h}", [P, KT_E, GS], F32R) for h in range(2)]
        kT = [m.sb(f"kT{h}", [P, KT_E, KPAD], F32R) for h in range(2)]
        lora_at = m.at
        v_raw = m.sb("v_raw", [P, 2, 3, E], F32)
        v_split = [m.sb(f"v_split{h}", [P, 3, E], F32R) for h in range(2)]
        mask_sb = m.sb("mask_sb", [P, 2, KEYS + 1], F32)
        logits = m.sb("logits", [P, 2, KEYS + 1], F32)
        probs = m.sb("probs", [P, 2, 3 * P], F32)
        pT = [m.sb(f"pT{h}", [P, 3, S], F32R) for h in range(2)]
        x_norm = m.sb("x_norm", [P, 2, E], F32)
        x_res = m.sb("x_res", [P, 2, E], F32)
        y_out = m.sb("y_out", [P, 2, E], F32)
        assert m.at <= nc.sbuf_usable_end, m.at
        lora_raw = Map(lora_at).sb("lora_raw", [P, 2 * (E + H)], F32)
        m = Map(phase_at)
        q_int = m.sb("q_int", [P, 2, 2, E], I32)
        w_real = m.sb("w_real", [P, 2, 2, E], F32)
        up_w = [[m.sb(f"up_w{n}_{h}", [P, KT_E, P], F32R) for h in range(2)] for n in range(EARLY)]
        down_w = [[m.sb(f"down_w{n}_{h}", [P, E], F32R) for h in range(2)] for n in range(EARLY)]
        assert m.at <= rows_at
        m = Map(rows_at)
        zT = [m.sb(f"zT{h}", [P, KT_E, CHUNK], F32R) for h in range(2)]
        hid_raw = m.sb("hid_raw", [P, CHUNK], F32)
        hid_high = [m.sb("hid_high0", [P, CHUNK], F32R)]
        assert m.at <= rest_at - 4 * GB * E
        y_in = Map(rest_at - 4 * GB * E).sb("y_in", [P, CT, E], F32)
        m = Map(rest_at)
        hid_high.append(m.sb("hid_high1", [P, CHUNK], F32R))
        hid_low = [m.sb(f"hid_low{n}", [P, CHUNK], F32R) for n in range(2)]
        hidT = [hid_high, hid_low]
        for n in range(EARLY, HT):
            up_w.append([m.sb(f"up_w{n}_{h}", [P, KT_E, P], F32R) for h in range(2)])
            down_w.append([m.sb(f"down_w{n}_{h}", [P, E], F32R) for h in range(2)])
        assert m.at <= nc.sbuf_usable_end, m.at

        ps = ctx.enter_context(nc.psum_tensor("ps", [P, 8, 512], F32))
        QK, LN_T, V_NEW, SCORES, P_T, AV = 0, 2, 3, 4, 5, 6
        LORA_UP, LORA_DOWN, HID, ACC = 0, 1, 3, (5, 6, 7, 2)
        Z_FIRST, Z_LATER = (7, 2), (0, 1)

        def sem(name):
            return ctx.enter_context(nc.semaphore(name))

        s_x = [sem(f"s_x{n}") for n in range(GB)]
        s_xres = [sem(f"s_xres{n}") for n in range(2)]
        s_kctx = [sem(f"s_kctx{n}") for n in range(GB)]
        s_vctx = [sem(f"s_vctx{n}") for n in range(2)]
        s_mask = [sem(f"s_mask{n}") for n in range(2)]
        s_wk = [sem(f"s_wk{n}") for n in range(KT_E)]
        s_w = {n: sem(f"s_w{n}") for n in (0, 2)}
        s_bias = sem("s_bias")
        s_lora_in = sem("s_lora_in")
        s_ymid = [sem(f"s_ymid{n}") for n in range(2)]
        s_y = [sem(f"s_y{n}") for n in range(CT)]
        s_res = [sem(f"s_res{n}") for n in range(CT)]
        s_q = [sem(f"s_q{n}") for n in range(2)]
        s_out = [sem(f"s_out{n}") for n in range(CT)]
        xt_t = sem("xt_t")
        kproj = sem("kproj")
        qproj = sem("qproj")
        vproj = sem("vproj")
        scored = sem("scored")
        p_t = sem("p_t")
        av_done = sem("av_done")
        z_t = sem("z_t")
        lora_up_done = sem("lora_up_done")
        lora_down_done = sem("lora_down_done")
        up_done = sem("up_done")
        down_done = sem("down_done")
        wk_hi = sem("wk_hi")
        w_hi = sem("w_hi")
        lora_hi = sem("lora_hi")
        xt_evac = sem("xt_evac")
        xt_hi = sem("xt_hi")
        k_evac = sem("k_evac")
        q_hi = sem("q_hi")
        k_hi = sem("k_hi")
        v_hi = sem("v_hi")
        exp_done = sem("exp_done")
        p_hi = sem("p_hi")
        z_hi = sem("z_hi")
        up_hi = sem("up_hi")
        down_hi = sem("down_hi")
        hid_real = sem("hid_real")
        hid_hi = sem("hid_hi")
        wk_lo = sem("wk_lo")
        w_lo = sem("w_lo")
        lora_lo = sem("lora_lo")
        bq_ready = sem("bq_ready")
        stats = sem("stats")
        stats_step = sem("stats_step")
        norm = sem("norm")
        xt_lo = sem("xt_lo")
        q_lo = sem("q_lo")
        k_lo = sem("k_lo")
        v_evac = sem("v_evac")
        v_lo = sem("v_lo")
        maxed = sem("maxed")
        soft = sem("soft")
        inv = sem("inv")
        p_lo = sem("p_lo")
        y_done = sem("y_done")
        z_lo = sem("z_lo")
        up_step = sem("up_step")
        down_step = sem("down_step")
        up_real = sem("up_real")
        down_real = sem("down_real")
        up_lo = sem("up_lo")
        down_lo = sem("down_lo")
        hid_lo = sem("hid_lo")
        out_done = sem("out_done")
        const_step = sem("const_step")
        const_ready = sem("const_ready")
        pads = sem("pads")
        lora_zero = sem("lora_zero")
        root = sem("root")
        res_ready = sem("res_ready")

        block = ctx.enter_context(nc.Block())

        LAST = GROUPS - 1

        def groups(eng, body):
            body(0, True, False)
            with eng.Fori(1, LAST) as g:
                body(g, False, False)
            body(LAST, False, True)

        def chunks(eng, body):
            body(0, CT, CT, True)
            with eng.Fori(1, FULL - 1) as c:
                body(c, CT, CT, False)
            body(FULL - 1, CT, REST, False)
            body(FULL, REST, 0, False)

        UP_A, UP_B, DOWN_A, DOWN_B = 0, E, E + H, E + 2 * H

        @block.sync
        def _(sp):
            def load_x(b, slot):
                sp.dma_start(x_in[0:S, slot, :], x[b]).then_inc(s_x[slot], 16)

            def load_mask(b, slot):
                sp.dma_start(mask_sb[0:S, slot, 0:KEYS], mask[b]).then_inc(s_mask[slot], 16)

            def load_k(b, i):
                sp.dma_start(k_raw[:, i, :, S:KEYS], ctx_k[b]).then_inc(s_kctx[i], 16)

            def load_v(b, slot):
                sp.dma_start(v_raw[S:P, slot, 0, :], ctx_v[b, 0:P - S, :]).then_inc(s_vctx[slot], 16)
                sp.dma_start(v_raw[:, slot, 1:3, :],
                             ctx_v[b, P - S:VROWS, :].rearrange("(t p) e -> p t e", p=P)).then_inc(s_vctx[slot], 16)

            def load_res(b, slot):
                sp.dma_start(x_res[0:S, slot, :], x[b]).then_inc(s_xres[slot], 16)

            load_x(0, 0)
            for k in range(KT_E):
                cols = slice(k * E, (k + 1) * E)
                sp.dma_start(w_stage[:, 1, cols], w_qkv[1, :, cols]).then_inc(s_wk[k], 16)
                if k == 0:
                    for b in range(1, GB):
                        load_x(b, b)
            sp.dma_start(bqk_col[:], b_qk).then_inc(s_bias, 16)
            sp.dma_start(w_stage[:, 0, :], w_qkv[0]).then_inc(s_w[0], 16)
            sp.dma_start(bup_col[:], b_up).then_inc(s_bias, 16)
            sp.dma_start(bv_row[:], b_v.partition_broadcast(P)).then_inc(s_bias, 16)
            sp.dma_start(bdown_row[:], b_down.partition_broadcast(P)).then_inc(s_bias, 16)
            sp.dma_start(w_stage[:, 2, :], w_qkv[2]).then_inc(s_w[2], 16)
            load_k(0, 0)
            sp.wait_ge(lora_zero, 1)
            for quadrant in range(4):
                sp.dma_start(lora_raw[quadrant * 32:quadrant * 32 + R, :], lora).then_inc(s_lora_in, 16)
            load_mask(0, 0)
            for i in range(1, GB):
                load_k(i, i)
            for i in range(GB):
                sp.wait_ge(norm, i + 1)
                load_x(GB + i, i)
            sp.wait_ge(lora_lo, 2)
            for b in range(2):
                load_v(b, b)

            def group(g, first, last):
                for i in range(0 if first else GB):
                    if not last:
                        sp.wait_ge(norm, g * GB + i + 1)
                        load_x(g * GB + GB + i, i)
                    else:
                        if i == 0:
                            sp.wait_ge(s_ymid[0], 16 * ((CHUNK - 1) // S // 2 + 1))
                            sp.wait_ge(s_ymid[1], 16 * (((CHUNK - 1) // S + 1) // 2))
                            sp.wait_ge(norm, B)
                        load_y(i, i)
                for i in range(GB):
                    b = g * GB + i
                    if not (first and i < 2):
                        sp.wait_ge(y_done, b - 1)
                    load_res(b, i % 2)
                    if not (first and i < 2):
                        sp.wait_ge(v_lo, b - 1)
                        load_v(b, i % 2)
                    if not (last and i == GB - 1):
                        if not (first and i == 0):
                            sp.wait_ge(maxed, b)
                        load_mask(b + 1, (i + 1) % 2)
                    if not (first and i == 0) and not (last and i > 0):
                        sp.wait_ge(k_lo, b)
                        load_k(b + GB - 1, (i - 1) % GB)
                    if last and i < EARLY:
                        if i == 0:
                            sp.wait_ge(qproj, GROUPS * KT_E)
                        load_w(i)

            def load_y(t, slot):
                sp.dma_start(y_in[:, slot, :], y_mid_rows[bass.ts(t, P), :]).then_inc(s_y[slot], 16)

            def load_w(n):
                k = n % 2
                sp.dma_start(q_int[:, k, 0, :], up_q[n]).then_inc(s_q[k], 16)
                sp.dma_start(q_int[:, k, 1, :], down_q[n]).then_inc(s_q[k], 16)
                for half in range(2):
                    rows = slice(half * (P // 2), (half + 1) * (P // 2))
                    sp.dma_start(w_real[rows, k, 0, :], up_s[half, n].partition_broadcast(P // 2)).then_inc(s_q[k], 16)
                    sp.dma_start(w_real[rows, k, 1, :], down_s[half, n].partition_broadcast(P // 2)).then_inc(s_q[k], 16)

            groups(sp, group)

            def next_rows(c, following):
                for j in range(following):
                    sp.wait_ge(z_t, c * CT + j + 1)
                    load_y(c * CT + CT + j, j)

            for n in range(EARLY, HT):
                if n == 4:
                    for k in range(2):
                        sp.wait_ge(s_ymid[k], 16 * (B // 2))
                    next_rows(0, CT)
                sp.wait_ge(up_lo, n - 1)
                sp.wait_ge(down_lo, n - 1)
                load_w(n)

            def chunk(c, tiles, following, first):
                if first:
                    sp.wait_ge(lora_up_done, HT)
                    sp.wait_ge(lora_down_done, HT)
                else:
                    next_rows(c, following)
                for j in range(tiles):
                    if not first:
                        sp.wait_ge(s_out[j], 16 * c)
                    sp.dma_start(y_res[:, j, :], y_mid_rows[bass.ts(c * CT + j, P), :]).then_inc(s_res[j], 16)

            chunks(sp, chunk)
            for j in range(CT):
                sp.wait_ge(s_out[j], 16 * (FULL + (j < REST)))

        @block.gpsimd
        def _(pool):
            pool.memset(ident[:], 0.0).then_inc(const_step, 1)
            pool.memset(minus_half[:], -0.5).then_inc(const_step, 1)
            pool.wait_ge(const_step, 2)
            pool.affine_select(out=ident[:], in_=ident[:], compare_op=ALU.not_equal, fill=1.0, base=0,
                               pattern=[[-1, P]], channel_multiplier=1).then_inc(const_ready, 1)
            pool.memset(lora_raw[:], 0.0).then_inc(lora_zero, 1)
            pool.memset(k_raw[:, :, :, KEYS:KPAD], 0.0).then_inc(pads, 1)
            pool.memset(probs[:, :, KEYS:3 * P], 0.0).then_inc(pads, 1)

            def inv_root(n, slot, rows):
                pool.wait_ge(stats, n + 1)
                pool.tensor_tensor(rstd[0:rows, slot, :], var_eps[0:rows, slot, :], minus_half[0:rows, :],
                                   ALU.pow).then_inc(root, 1)

            for b in range(GB):
                inv_root(b, b % 2, S)

            def store_mid(b, slot):
                pool.wait_ge(y_done, b + 1)
                pool.dma_start(y_mid[b], y_out[0:S, slot, :]).then_inc(s_ymid[slot], 16)

            def group(g, first, last):
                if not first:
                    store_mid(g * GB - 2, 0)
                for i in range(GB):
                    if i == 2 and not first:
                        store_mid(g * GB - 1, 1)
                    inv_root(g * GB + GB + i, i % 2, P if last else S)
                for i in range(GB - 2):
                    store_mid(g * GB + i, i % 2)

            groups(pool, group)
            store_mid(B - 2, 0)
            store_mid(B - 1, 1)

            def chunk(c, tiles, following, first):
                for j in range(following):
                    inv_root(c * CT + (B + CT + j), j % 2, P)
                for j in range(tiles):
                    pool.wait_ge(s_res[j], 16 * c + 16)
                    pool.tensor_tensor(y_res[:, j, :], y_res[:, j, :], bdown_row[:], ALU.add).then_inc(res_ready, 1)
                for j in range(tiles):
                    pool.wait_ge(out_done, c * CT + j + 1)
                    pool.dma_start(out[bass.ts(c * CT + j, P), :], y_res[:, j, :]).then_inc(s_out[j], 16)

            chunks(pool, chunk)

        @block.scalar
        def _(act):
            def w_high(which):
                act.wait_ge(s_w[which], 16)
                high = wv_split[0][:] if which == 2 else qk_split[0][:, which, :, :]
                act.activation(high.rearrange("p k f -> p (k f)"), w_stage[:, which, :],
                               ACT.Copy, scale=SCALE if which == 0 else 1.0).then_inc(w_hi, 1)

            def xt_evacuate(b, i):
                act.wait_ge(xt_t, b + 1)
                act.activation(xT_next[:, :, i * S:(i + 1) * S],
                               ps[:, LN_T, 0:KT_E * S].rearrange("p (k s) -> p k s", k=KT_E),
                               ACT.Copy).then_inc(xt_evac, 1)

            def v_high(b, half_b, slot):
                act.wait_ge(v_evac, b + 1)
                act.wait_ge(s_vctx[slot], half_b * 32 + 32)
                act.wait_ge(av_done, b)
                act.activation(v_split[0][:], v_raw[:, slot, :, :], ACT.Copy).then_inc(v_hi, 1)

            def v_high_first():
                act.wait_ge(v_evac, 1)
                act.wait_ge(s_vctx[0], 32)
                act.activation(v_split[0][:], v_raw[:, 0, :, :], ACT.Copy).then_inc(v_hi, 1)

            def p_high(b, first):
                act.wait_ge(p_t, b + 1)
                if not first:
                    act.wait_ge(av_done, b)
                act.activation(pT[0][:].rearrange("p t s -> p (t s)"), ps[:, P_T, 0:3 * S],
                               ACT.Copy).then_inc(p_hi, 1)

            def k_high(g, i, first):
                b = g * GB + i
                act.wait_ge(k_evac, g * KT_E + KT_E)
                act.wait_ge(s_kctx[i], 16 * g + 16)
                if first and i == 0:
                    act.wait_ge(pads, 2)
                else:
                    act.wait_ge(scored, b)
                act.activation(kT[0][:], k_raw[:, i, :, :], ACT.Copy).then_inc(k_hi, 1)

            for k in range(KT_E):
                act.wait_ge(s_wk[k], 16)
                act.activation(qk_split[0][:, 1, k, :], w_stage[:, 1, k * E:(k + 1) * E], ACT.Copy).then_inc(wk_hi, 1)
            for i in range(GB):
                xt_evacuate(i, i)

            def group(g, first, last):
                for k in range(KT_E):
                    if first and k == 0:
                        act.wait_ge(xt_evac, GB)
                    elif k == 0:
                        act.wait_ge(xt_evac, g * GB + GB)
                        act.wait_ge(vproj, g * GB)
                    act.activation(xT[0][:, k, :], xT_next[:, k, :], ACT.Copy).then_inc(xt_hi, 1)
                if not first:
                    v_high(g * GB - 1, g * 2 - 1, 1)
                    p_high(g * GB - 1, False)
                for f in range(KT_E):
                    if first and f < 2:
                        w_high(2 * f)
                    elif first:
                        if f == 2:
                            act.wait_ge(s_lora_in, 64)
                            act.wait_ge(wk_lo, KT_E)
                            act.wait_ge(w_lo, 2)
                        cols = slice((f - 2) * (E + H), (f - 1) * (E + H))
                        act.activation(lora_w[:, cols], lora_raw[:, cols], ACT.Copy).then_inc(lora_hi, 1)
                    if first and f == 0:
                        act.wait_ge(s_bias, 64)
                    act.wait_ge(kproj, g * KT_E + f + 1)
                    if not first:
                        act.wait_ge(k_lo, g * GB)
                    act.activation(k_raw[:, :, f, 0:S],
                                   ps[:, QK + f % 2, 0:GS].rearrange("p (b s) -> p b s", b=GB),
                                   ACT.Identity, bias=bqk_col[:, KT_E + f:KT_E + f + 1]).then_inc(k_evac, 1)
                k_high(g, 0, first)
                if first:
                    act.wait_ge(bq_ready, 1)
                for f in range(KT_E):
                    act.wait_ge(qproj, g * KT_E + f + 1)
                    act.activation(qT[0][:, f, :], ps[:, QK + f % 2, 0:GS], ACT.Identity,
                                   bias=bq_scaled[:, f:f + 1]).then_inc(q_hi, 1)
                    if not last:
                        if f == 0:
                            act.wait_ge(xt_lo, g * KT_E + KT_E)
                        xt_evacuate(g * GB + GB + f, f)
                for i in range(GB):
                    b = g * GB + i
                    if i == 1 and first:
                        v_high_first()
                        p_high(0, True)
                    elif i > 0:
                        v_high(b - 1, g * 2 + (i - 1) // 2, (i - 1) % 2)
                        p_high(b - 1, False)
                    if i < GB - 1:
                        k_high(g, i + 1, first)
                    act.wait_ge(soft, b + 1)
                    if not (first and i < 2):
                        act.wait_ge(p_t, b - 1)
                        act.wait_ge(inv, b - 1)
                    act.activation(probs[0:S, i % 2, 0:KEYS], logits[0:S, i % 2, 0:KEYS], ACT.Exp,
                                   bias=minus_max[0:S, i % 2, :],
                                   accum_out=row_sum[0:S, i % 2, :]).then_inc(exp_done, 1)
                    if last and 1 <= i <= EARLY:
                        up_high(i - 1)
                        down_high(i - 1)

            def z_high(t, j, banks):
                act.wait_ge(z_t, t + 1)
                act.activation(zT[0][:, :, j * P:(j + 1) * P],
                               ps[:, banks[j % 2], :].rearrange("p (k s) -> p k s", k=KT_E),
                               ACT.Copy).then_inc(z_hi, 1)

            def hidden(c, n, width, first):
                act.wait_ge(up_done, c * HT + n + 1)
                if not (first and n == 0):
                    act.wait_ge(hid_lo, c * HT + n)
                act.activation(hid_raw[:, 0:width], ps[:, HID + n % 2, 0:width], ACT.Relu,
                               bias=bup_col[:, n:n + 1]).then_inc(hid_real, 1)
                if not (first and n < 2):
                    act.wait_ge(down_done, c * HT + n - 1)
                act.activation(hidT[0][n % 2][:, 0:width], ps[:, HID + n % 2, 0:width], ACT.Relu,
                               bias=bup_col[:, n:n + 1]).then_inc(hid_hi, 1)

            def up_high(n):
                act.wait_ge(up_real, n + 1)
                act.activation(up_w[n][0][:].rearrange("p k h -> p (k h)"), w_real[:, n % 2, 0, :],
                               ACT.Copy).then_inc(up_hi, 1)

            def down_high(n):
                act.wait_ge(down_real, n + 1)
                act.activation(down_w[n][0][:], w_real[:, n % 2, 1, :], ACT.Copy).then_inc(down_hi, 1)

            groups(act, group)
            for j in range(2):
                z_high(j, j, Z_FIRST)
            p_high(B - 1, False)
            for j in range(2, CT):
                z_high(j, j, Z_FIRST)
            v_high(B - 1, B // 2 - 1, 1)

            def chunk(c, tiles, following, first):
                for n in range(HT):
                    if first and n + EARLY < HT:
                        if n == 1:
                            act.wait_ge(y_done, B)
                            for k in range(2):
                                act.wait_ge(s_ymid[k], 16 * (B // 2))
                        up_high(n + EARLY)
                    hidden(c, n, tiles * P, first)
                    if first and n + EARLY < HT:
                        down_high(n + EARLY)
                for j in range(following):
                    if j == 0:
                        act.wait_ge(up_done, c * HT + HT)
                    z_high(c * CT + CT + j, j, Z_LATER)

            chunks(act, chunk)

        @block.vector
        def _(dve):
            def ln_stats(n, src, slot, rows):
                dve.bn_stats(bn_raw[0:rows, slot, :], src).then_inc(stats_step, 1)
                dve.wait_ge(stats_step, 2 * n + 1)
                dve.memset(gate[:], 0.0)
                dve.bn_aggr(mean_var[0:rows, slot, :], bn_raw[0:rows, slot, :]).then_inc(stats_step, 1)
                dve.wait_ge(stats_step, 2 * n + 2)
                dve.tensor_scalar(var_eps[0:rows, slot, :], mean_var[0:rows, slot, 1:2], EPS, None,
                                  ALU.add).then_inc(stats, 1)

            def ln_apply(n, dst, src, slot, rows):
                dve.wait_ge(root, n + 1)
                dve.tensor_scalar(dst, src, mean_var[0:rows, slot, 0:1], rstd[0:rows, slot, :],
                                  ALU.subtract, ALU.mult).then_inc(norm, 1)

            def x_stats(g, i):
                dve.wait_ge(s_x[i], g * 16 + 16)
                ln_stats(g * GB + i, x_in[0:S, i, :], i % 2, S)

            def x_apply(b, i, fresh):
                if not fresh:
                    dve.wait_ge(xt_t, b - 1)
                ln_apply(b, x_norm[0:S, i % 2, :], x_in[0:S, i, :], i % 2, S)

            def w_low(which, n):
                dve.wait_ge(w_hi, n + 1)
                hi, lo = ((wv_split[h][:] if which == 2 else qk_split[h][:, which, :, :]).rearrange("p k f -> p (k f)")
                          for h in range(2))
                hi = hi.bitcast(F32)
                dve.scalar_tensor_tensor(lo, w_stage[:, which, :], SCALE if which == 0 else 1.0, hi,
                                         ALU.mult, ALU.subtract).then_inc(w_lo, 1)

            for b in range(0, GB, 2):
                x_stats(0, b)
                x_stats(0, b + 1)
                x_apply(b, b, b < 2)
                x_apply(b + 1, b + 1, b < 2)
            for k in range(KT_E):
                dve.wait_ge(wk_hi, k + 1)
                dve.tensor_tensor(qk_split[1][:, 1, k, :], w_stage[:, 1, k * E:(k + 1) * E],
                                  qk_split[0][:, 1, k, :].bitcast(F32), ALU.subtract).then_inc(wk_lo, 1)

            def v_evacuate(b, slot, fresh):
                dve.wait_ge(vproj, b + 1)
                if not fresh:
                    dve.wait_ge(v_lo, b - 1)
                dve.tensor_tensor(v_raw[0:S, slot, 0, :], ps[0:S, V_NEW, :], bv_row[0:S, :],
                                  ALU.add).then_inc(v_evac, 1)

            def v_low(b, slot):
                dve.wait_ge(v_hi, b + 1)
                dve.tensor_tensor(v_split[1][:], v_raw[:, slot, :, :], v_split[0][:].bitcast(F32),
                                  ALU.subtract).then_inc(v_lo, 1)

            def p_low(b):
                dve.wait_ge(p_hi, b + 1)
                dve.tensor_tensor(pT[1][:].rearrange("p t s -> p (t s)"), ps[:, P_T, 0:3 * S],
                                  pT[0][:].rearrange("p t s -> p (t s)").bitcast(F32),
                                  ALU.subtract).then_inc(p_lo, 1)

            def k_low(b, i):
                dve.wait_ge(k_hi, b + 1)
                dve.tensor_tensor(kT[1][:], k_raw[:, i, :, :], kT[0][:].bitcast(F32),
                                  ALU.subtract).then_inc(k_lo, 1)

            def softmax_shift(b, half_b, slot, fresh):
                dve.wait_ge(scored, b + 1)
                dve.wait_ge(s_mask[slot], half_b * 16 + 16)
                if not fresh:
                    dve.wait_ge(exp_done, b - 1)
                dve.memset(gate[:], 0.0)
                dve.tensor_tensor_reduce(logits[0:S, slot, 0:KEYS], ps[0:S, SCORES, 0:KEYS],
                                         mask_sb[0:S, slot, 0:KEYS], 1.0, -3.0e38, ALU.add, ALU.max,
                                         row_max[0:S, slot, :]).then_inc(maxed, 1)
                dve.wait_ge(maxed, b + 1)
                dve.tensor_scalar(minus_max[0:S, slot, :], row_max[0:S, slot, :], -1.0, None,
                                  ALU.mult).then_inc(soft, 1)

            def attended(b, half_b, slot, fresh):
                dve.wait_ge(exp_done, b + 1)
                dve.reciprocal(inv_sum[0:S, slot, :], row_sum[0:S, slot, :]).then_inc(inv, 1)
                dve.wait_ge(inv, b + 1)
                dve.wait_ge(av_done, b + 1)
                dve.wait_ge(s_xres[slot], half_b * 16 + 16)
                if not fresh:
                    dve.wait_ge(s_ymid[slot], half_b * 16)
                dve.scalar_tensor_tensor(y_out[0:S, slot, :], ps[0:S, AV, :], inv_sum[0:S, slot, :],
                                         x_res[0:S, slot, :], ALU.mult, ALU.add).then_inc(y_done, 1)

            def lora_low(half):
                dve.wait_ge(lora_hi, half + 1)
                a, b, na, nb = ((UP_A, UP_B, E, H), (DOWN_A, DOWN_B, H, E))[half]
                for at, rows, n in ((a, slice(64, 128), na), (b, slice(32, 64), nb), (b, slice(96, 128), nb)):
                    part = lora_w[rows, at:at + n]
                    low = dve.tensor_tensor(part, lora_raw[rows, at:at + n], part.bitcast(F32), ALU.subtract)
                low.then_inc(lora_lo, 1)

            def rows_stats(g, i, last):
                if last:
                    y_stats(i, 16, i % 2, i)
                else:
                    x_stats(g + 1, i)

            def rows_apply(g, i, last):
                if last:
                    y_apply(i, i % 2, i)
                else:
                    x_apply(g * GB + GB + i, i, False)

            def group(g, first, last):
                for k in range(KT_E):
                    dve.wait_ge(xt_hi, g * KT_E + k + 1)
                    dve.tensor_tensor(xT[1][:, k, :], xT_next[:, k, :], xT[0][:, k, :].bitcast(F32),
                                      ALU.subtract).then_inc(xt_lo, 1)
                if first:
                    w_low(0, 0)
                    w_low(2, 1)
                    dve.wait_ge(s_bias, 64)
                    dve.tensor_scalar(bq_scaled[:], bqk_col[:, 0:KT_E], SCALE, None, ALU.mult).then_inc(bq_ready, 1)
                else:
                    attended(g * GB - 2, g * 2 - 1, 0, False)
                    v_low(g * GB - 1, 1)
                    p_low(g * GB - 1)
                rows_stats(g, 0, last)
                rows_stats(g, 1, last)
                rows_apply(g, 0, last)
                rows_apply(g, 1, last)
                if first:
                    lora_low(0)
                else:
                    attended(g * GB - 1, g * 2 - 1, 1, False)
                k_low(g * GB, 0)
                rows_stats(g, 2, last)
                rows_stats(g, 3, last)
                for f in range(KT_E):
                    dve.wait_ge(q_hi, g * KT_E + f + 1)
                    dve.scalar_tensor_tensor(qT[1][:, f, :], ps[:, QK + f % 2, 0:GS], bq_scaled[:, f:f + 1],
                                             qT[0][:, f, :].bitcast(F32), ALU.add, ALU.subtract).then_inc(q_lo, 1)
                    if f < 2:
                        rows_apply(g, 2 + f, last)
                if first:
                    lora_low(1)
                for i in range(GB):
                    b = g * GB + i
                    if i > 0:
                        v_low(b - 1, (i - 1) % 2)
                        p_low(b - 1)
                    softmax_shift(b, g * 2 + i // 2, i % 2, first and i < 2)
                    if i < GB - 1:
                        k_low(b + 1, i + 1)
                    v_evacuate(b, i % 2, first and i < 2)
                    if 0 < i < GB - 1:
                        attended(b - 1, g * 2, i - 1, first)
                    if last and 1 <= i <= EARLY:
                        prepare(i - 1)

            def y_stats(t, c16, slot, j):
                dve.wait_ge(s_y[j], c16)
                ln_stats(t + B, y_in[:, j, :], slot, P)

            def y_apply(t, slot, j):
                ln_apply(t + B, y_in[:, j, :], y_in[:, j, :], slot, P)

            def z_low(t, j, banks):
                dve.wait_ge(z_hi, t + 1)
                dve.tensor_tensor(zT[1][:, :, j * P:(j + 1) * P],
                                  ps[:, banks[j % 2], :].rearrange("p (k s) -> p k s", k=KT_E),
                                  zT[0][:, :, j * P:(j + 1) * P].bitcast(F32), ALU.subtract).then_inc(z_lo, 1)

            def prepare(n):
                k = n % 2
                dve.wait_ge(s_q[k], 96 * (n // 2) + 96)
                for part, bank, step, real, product in ((0, LORA_UP, up_step, up_real, lora_up_done),
                                                        (1, LORA_DOWN, down_step, down_real, lora_down_done)):
                    w = w_real[:, k, part, :]
                    dve.scalar_tensor_tensor(w, q_int[:, k, part, :], -ZERO_POINT, w,
                                             ALU.add, ALU.mult).then_inc(step, 1)
                    dve.wait_ge(step, n + 1)
                    dve.wait_ge(product, n + 1)
                    dve.tensor_tensor(w, ps[:, bank, :], w, ALU.add).then_inc(real, 1)
                dve.wait_ge(up_hi, n + 1)
                dve.tensor_tensor(up_w[n][1][:].rearrange("p k h -> p (k h)"), w_real[:, k, 0, :],
                                  up_w[n][0][:].rearrange("p k h -> p (k h)").bitcast(F32),
                                  ALU.subtract).then_inc(up_lo, 1)
                dve.wait_ge(down_hi, n + 1)
                dve.tensor_tensor(down_w[n][1][:], w_real[:, k, 1, :], down_w[n][0][:].bitcast(F32),
                                  ALU.subtract).then_inc(down_lo, 1)

            groups(dve, group)
            for j in range(2):
                z_low(j, j, Z_FIRST)
            attended(B - 2, B // 2 - 1, 0, False)
            p_low(B - 1)
            for j in range(2, CT):
                z_low(j, j, Z_FIRST)
            v_low(B - 1, 1)

            def chunk(c, tiles, following, first):
                for n in range(HT):
                    if first and n + EARLY < HT:
                        prepare(n + EARLY)
                    if first and n == 0:
                        attended(B - 1, B // 2 - 1, 1, False)
                    if n % 2 == 0 and n >= HT // 2 and (n - HT // 2) // 2 < following:
                        j = (n - HT // 2) // 2
                        y_stats(c * CT + (CT + j), 16 * c + 32, j % 2, j)
                    dve.wait_ge(hid_hi, c * HT + n + 1)
                    if not (first and n < 2):
                        dve.wait_ge(down_done, c * HT + n - 1)
                    dve.tensor_tensor(hidT[1][n % 2][:, 0:tiles * P], hid_raw[:, 0:tiles * P],
                                      hidT[0][n % 2][:, 0:tiles * P].bitcast(F32), ALU.subtract).then_inc(hid_lo, 1)
                    if n % 2 == 0 and n >= HT // 2 and (n - HT // 2) // 2 < following:
                        j = (n - HT // 2) // 2
                        y_apply(c * CT + (CT + j), j % 2, j)
                for j in range(following):
                    z_low(c * CT + (CT + j), j, Z_LATER)
                for j in range(tiles):
                    dve.wait_ge(down_done, c * HT + HT)
                    dve.wait_ge(res_ready, c * CT + j + 1)
                    dve.tensor_tensor(y_res[:, j, :], ps[:, ACC[j], :], y_res[:, j, :], ALU.add).then_inc(out_done, 1)

            chunks(dve, chunk)

        @block.tensor
        def _(pe):
            def product(dst, lhs, rhs, steps, done=None):
                n = len(PASSES) * steps
                for s in range(steps):
                    for a, b in PASSES:
                        i = s * len(PASSES) + PASSES.index((a, b))
                        last = pe.matmul(dst, lhs(a, s), rhs(b, s), start=(i == 0), stop=(i == n - 1))
                if done is not None:
                    last.then_inc(done, 1)

            def x_transpose(b, slot, fresh):
                pe.wait_ge(norm, b + 1)
                if not fresh:
                    pe.wait_ge(xt_evac, b)
                for k in range(KT_E):
                    last = pe.transpose(ps[:, LN_T, k * S:(k + 1) * S], x_norm[0:S, slot, k * P:(k + 1) * P],
                                        ident[0:S, 0:S])
                last.then_inc(xt_t, 1)

            def p_transpose(b, slot, fresh):
                pe.wait_ge(exp_done, b + 1)
                if fresh:
                    pe.wait_ge(pads, 2)
                else:
                    pe.wait_ge(p_lo, b)
                for t in range(3):
                    last = pe.transpose(ps[:, P_T, t * S:(t + 1) * S], probs[0:S, slot, t * P:(t + 1) * P],
                                        ident[0:S, 0:S])
                last.then_inc(p_t, 1)

            def attend(b, fresh):
                pe.wait_ge(p_lo, b + 1)
                pe.wait_ge(v_lo, b + 1)
                if not fresh:
                    pe.wait_ge(y_done, b)
                product(ps[0:S, AV, :], lambda h, t: pT[h][:, t, :], lambda h, t: v_split[h][:, t, :], 3, av_done)

            pe.wait_ge(const_ready, 1)
            for b in range(GB):
                x_transpose(b, b % 2, b == 0)

            def group(g, first, last):
                for which, done in ((1, kproj), (0, qproj)):
                    if first and which == 0:
                        pe.wait_ge(w_lo, 1)
                    for f in range(KT_E):
                        if which == 1 and f < 2 and not first:
                            pe.wait_ge(q_lo, g * KT_E - 1 + f)
                        elif which == 1 and f >= 2:
                            pe.wait_ge(k_evac, g * KT_E + f - 1)
                        elif which == 0 and f < 2:
                            pe.wait_ge(k_evac, g * KT_E + f + 3)
                        elif which == 0:
                            pe.wait_ge(q_lo, g * KT_E + f - 1)
                        for k in range(KT_E):
                            if which == 1 and f == 0:
                                pe.wait_ge(xt_lo, g * KT_E + k + 1)
                                if first:
                                    pe.wait_ge(wk_lo, k + 1)
                            for a, b in PASSES:
                                mm = pe.matmul(ps[:, QK + f % 2, 0:GS],
                                               qk_split[a][:, which, k, f * P:(f + 1) * P], xT[b][:, k, :],
                                               start=(k == 0 and (a, b) == PASSES[0]),
                                               stop=(k == KT_E - 1 and (a, b) == PASSES[-1]))
                        mm.then_inc(done, 1)
                        if which == 0 and not last:
                            x_transpose(g * GB + GB + f, f % 2, False)
                    if which == 1 and not first:
                        attend(g * GB - 1, False)
                for i in range(GB):
                    b = g * GB + i
                    pe.wait_ge(k_lo, b + 1)
                    pe.wait_ge(q_lo, g * KT_E + KT_E)
                    if not (first and i == 0):
                        pe.wait_ge(maxed, b)
                    product(ps[0:S, SCORES, 0:KPAD], lambda h, k: qT[h][:, k, i * S:(i + 1) * S],
                            lambda h, k: kT[h][:, k, :], KT_E, scored)
                    if first and i == 0:
                        pe.wait_ge(w_lo, 2)
                    else:
                        pe.wait_ge(v_evac, b)
                    product(ps[0:S, V_NEW, :], lambda h, k: xT[h][:, k, i * S:(i + 1) * S],
                            lambda h, k: wv_split[h][:, k, :], KT_E, vproj)
                    if last and i == GB - 1:
                        for j in range(2):
                            z_transpose(j, j, True, Z_FIRST)
                    if i > 0:
                        attend(b - 1, first and i == 1)
                    p_transpose(b, i % 2, first and i == 0)
                    if last and 1 <= i <= EARLY:
                        lora_products(i - 1)

            def z_transpose(t, j, fresh, banks):
                pe.wait_ge(norm, t + B + 1)
                if not fresh:
                    pe.wait_ge(z_lo, t - 1)
                for k in range(KT_E):
                    last = pe.transpose(ps[:, banks[j % 2], k * P:(k + 1) * P], y_in[:, j, k * P:(k + 1) * P], ident[:])
                last.then_inc(z_t, 1)

            def lora_products(n):
                pe.wait_ge(q_lo, GROUPS * KT_E)
                if n > 0:
                    pe.wait_ge(up_real, n)
                for k in range(KT_E):
                    last = pe.matmul(ps[:, LORA_UP, k * P:(k + 1) * P], lora_w[:, UP_A + k * P:UP_A + (k + 1) * P],
                                     lora_w[:, UP_B + n * P:UP_B + (n + 1) * P], start=True, stop=True)
                last.then_inc(lora_up_done, 1)
                if n > 0:
                    pe.wait_ge(down_real, n)
                pe.matmul(ps[:, LORA_DOWN, :], lora_w[:, DOWN_A + n * P:DOWN_A + (n + 1) * P],
                          lora_w[:, DOWN_B:DOWN_B + E], start=True, stop=True).then_inc(lora_down_done, 1)

            def up(c, n, width, first):
                if first:
                    pe.wait_ge(up_lo, n + 1)
                if not (first and n < 2):
                    pe.wait_ge(hid_hi, c * HT + n - 1)
                product(ps[:, HID + n % 2, 0:width], lambda h, k: up_w[n][h][:, k, :],
                        lambda h, k: zT[h][:, k, 0:width], KT_E, up_done)

            def down(c, n, tiles, first):
                if first:
                    pe.wait_ge(down_lo, n + 1)
                pe.wait_ge(hid_lo, c * HT + n + 1)
                for j in range(tiles):
                    if n == 0 and not first:
                        pe.wait_ge(out_done, (c - 1) * CT + j + 1)
                    for a, b in PASSES:
                        mm = pe.matmul(ps[:, ACC[j], :], hidT[a][n % 2][:, j * P:(j + 1) * P], down_w[n][b][:],
                                       start=(n == 0 and (a, b) == PASSES[0]),
                                       stop=(n == HT - 1 and (a, b) == PASSES[-1]))
                mm.then_inc(down_done, 1)


            groups(pe, group)
            for j in range(2, CT):
                z_transpose(j, j, False, Z_FIRST)

            def chunk(c, tiles, following, first):
                for n in range(HT):
                    if first and n + EARLY < HT:
                        lora_products(n + EARLY)
                    if n == 0:
                        pe.wait_ge(z_lo, c * CT + tiles)
                    if first and n == 0:
                        pe.wait_ge(v_evac, B)
                    if first and n == 1:
                        pe.wait_ge(maxed, B)
                    up(c, n, tiles * P, first)
                    if first and n == 0:
                        attend(B - 1, False)
                    if first and n == 1:
                        pe.wait_ge(y_done, B)
                    if n > 0:
                        down(c, n - 1, tiles, first)
                if first:
                    pe.wait_ge(up_real, HT)
                    pe.wait_ge(down_real, HT)
                for j in range(min(2, following)):
                    z_transpose(c * CT + (CT + j), j, False, Z_LATER)
                down(c, HT - 1, tiles, first)
                for j in range(2, following):
                    z_transpose(c * CT + (CT + j), j, False, Z_LATER)

            chunks(pe, chunk)


def kernel(x, ctx_2048, mask_BxSxS2_ff0, L0_xattn_Wq, L0_xattn_bq, L0_xattn_Wk, L0_xattn_bk, L0_xattn_Wv,
           L0_xattn_bv, L0_ffn_w_up_q, L0_ffn_w_up_scale, L0_ffn_b_up, L0_ffn_w_up_lora_a, L0_ffn_w_up_lora_b,
           L0_ffn_w_down_q, L0_ffn_w_down_scale, L0_ffn_b_down, L0_ffn_w_down_lora_a, L0_ffn_w_down_lora_b):
    import concourse.bacc as bacc
    import numpy as np
    from concourse.bass_utils import run_bass_kernel_spmd

    x, ctx, mask = (np.asarray(a) for a in (x, ctx_2048, mask_BxSxS2_ff0))
    tail = ctx[:, :CTX]
    mask = np.concatenate([mask[:, :, CTX:], mask[:, :, :CTX]], axis=2)
    ctx_k = tail.reshape(B, CTX, KT_E, P).transpose(0, 3, 2, 1)
    ctx_v = np.zeros((B, VROWS, E), ctx.dtype)
    ctx_v[:, :CTX] = tail
    w_qkv = np.stack([np.asarray(w).reshape(E, KT_E, P).transpose(2, 1, 0).reshape(P, KT_E * E)
                      for w in (L0_xattn_Wq, L0_xattn_Wk, L0_xattn_Wv)])
    b_qk = np.concatenate([np.asarray(b).reshape(KT_E, P).T for b in (L0_xattn_bq, L0_xattn_bk)], axis=1)
    per = P // 64
    up_q = np.asarray(L0_ffn_w_up_q).reshape(HT, P, KT_E, P).transpose(0, 3, 2, 1).reshape(HT, P, E)
    up_s = np.asarray(L0_ffn_w_up_scale).reshape(HT, P, KT_E, per).transpose(3, 0, 2, 1).reshape(per, HT, E)
    down_q = np.asarray(L0_ffn_w_down_q).reshape(E, HT, P).transpose(1, 2, 0)
    down_s = np.asarray(L0_ffn_w_down_scale).reshape(E, HT, per).transpose(2, 1, 0)
    lora = np.concatenate([np.asarray(L0_ffn_w_up_lora_a).T, np.asarray(L0_ffn_w_up_lora_b),
                           np.asarray(L0_ffn_w_down_lora_a).T, np.asarray(L0_ffn_w_down_lora_b)], axis=1)
    arrays = {
        "x": x, "mask": mask, "ctx_k": ctx_k, "ctx_v": ctx_v, "w_qkv": w_qkv, "b_qk": b_qk,
        "b_v": np.asarray(L0_xattn_bv), "up_q": up_q, "up_s": up_s,
        "b_up": np.asarray(L0_ffn_b_up).reshape(HT, P).T, "down_q": down_q, "down_s": down_s,
        "b_down": np.asarray(L0_ffn_b_down), "lora": lora,
    }
    arrays = {f"in_{name}": np.ascontiguousarray(a) for name, a in arrays.items()}
    nc = bacc.Bacc("TRN2", target_bir_lowering=False, num_devices=1)
    args = {name[3:]: nc.dram_tensor(name, a.shape, mybir.dt.from_np(a.dtype), kind="ExternalInput").ap()
            for name, a in arrays.items()}
    y_mid = nc.dram_tensor("y_mid", (B, S, E), F32, kind="Internal").ap()
    out = nc.dram_tensor("out_0", (B * S, E), F32, kind="ExternalOutput").ap()
    build(nc, y_mid=y_mid, y_mid_rows=y_mid.rearrange("b s e -> (b s) e"), out=out, **args)
    result = run_bass_kernel_spmd(nc, [arrays], core_ids=[0])
    return result.results[0]["out_0"].reshape(B, S, E)
```

```python
from contextlib import ExitStack

import concourse.bass as bass
from concourse import mybir

ALU = mybir.AluOpType
ACT = mybir.ActivationFunctionType
F32 = mybir.dt.float32
F32R = mybir.dt.float32r
I32 = mybir.dt.int32

P = 128
B, S, E = 16, 112, 512
CTX = 263
KEYS = S + CTX
KPAD = KEYS + 1
VROWS = 3 * P - S
H, R = 2048, 16
KT_E = E // P
GB = 4
GS = GB * S
GROUPS = B // GB
HT = H // P
CHUNK = 512
TILES = B * S // P
CT = CHUNK // P
FULL = TILES // CT
REST = TILES - FULL * CT
EPS = 1e-5
SCALE = float(E) ** -0.5
ZERO_POINT = 7.5
EARLY = 2
PASSES = ((0, 0), (0, 1), (1, 0))


def build(nc, x, mask, ctx_k, ctx_v, w_qkv, b_qk, b_v, up_q, up_s, b_up, down_q, down_s, b_down,
          lora, y_mid, y_mid_rows, out):
    with ExitStack() as ctx:
        base = nc.sbuf_base

        class Map:
            def __init__(self, at):
                self.at = at

            def sb(self, name, shape, dt):
                size = 4
                for n in shape[1:]:
                    size *= n
                t = nc.alloc_sbuf_tensor_at(name, shape, dt, offset=self.at)
                self.at += (size + 31) // 32 * 32
                return t

        base = (base + 31) // 32 * 32
        m = Map(base)
        ident = m.sb("ident", [P, P], F32)
        bdown_row = m.sb("bdown_row", [P, E], F32)
        bqk_col = m.sb("bqk_col", [P, 2 * KT_E], F32)
        bq_scaled = m.sb("bq_scaled", [P, KT_E], F32)
        bup_col = m.sb("bup_col", [P, HT], F32)
        bn_raw = m.sb("bn_raw", [P, GB, 6], F32)
        mean_var = m.sb("mean_var", [P, GB, 2], F32)
        var_eps = m.sb("var_eps", [P, GB, 1], F32)
        minus_half = m.sb("minus_half", [P, 1], F32)
        gate = m.sb("gate", [P, 1], F32)
        rstd = m.sb("rstd", [P, GB, 1], F32)
        row_max = m.sb("row_max", [P, 2, 1], F32)
        minus_max = m.sb("minus_max", [P, 2, 1], F32)
        row_sum = m.sb("row_sum", [P, 2, 1], F32)
        inv_sum = m.sb("inv_sum", [P, 2, 1], F32)
        stage_at = m.at
        w_stage = m.sb("w_stage", [P, 3, KT_E * E], F32)
        phase_at = m.at
        m = Map(stage_at)
        lora_w = m.sb("lora_w", [P, 2 * (E + H)], F32R)
        y_res = Map(stage_at).sb("y_res", [P, CT, E], F32)
        m = Map(phase_at)
        qk_split = [m.sb(f"qk_split{h}", [P, 2, KT_E, E], F32R) for h in range(2)]
        rows_at = m.at
        xT = [m.sb(f"xT{h}", [P, KT_E, GS], F32R) for h in range(2)]
        xT_next = m.sb("xT_next", [P, KT_E, GS], F32)
        x_in = m.sb("x_in", [P, GB, E], F32)
        rest_at = m.at
        bv_row = m.sb("bv_row", [P, E], F32)
        k_raw = m.sb("k_raw", [P, GB, KT_E, KPAD], F32)
        wv_split = [m.sb(f"wv_split{h}", [P, KT_E, E], F32R) for h in range(2)]
        qT = [m.sb(f"qT{h}", [P, KT_E, GS], F32R) for h in range(2)]
        kT = [m.sb(f"kT{h}", [P, KT_E, KPAD], F32R) for h in range(2)]
        v_raw = m.sb("v_raw", [P, 2, 3, E], F32)
        lora_at = m.at - 4 * 3 * E
        v_split = [m.sb(f"v_split{h}", [P, 3, E], F32R) for h in range(2)]
        y_out = m.sb("y_out", [P, 2, E], F32)
        mask_sb = m.sb("mask_sb", [P, 2, KEYS + 1], F32)
        logits = m.sb("logits", [P, 2, KEYS + 1], F32)
        probs = m.sb("probs", [P, 2, 3 * P], F32)
        pT = [m.sb(f"pT{h}", [P, 3, S], F32R) for h in range(2)]
        x_norm = m.sb("x_norm", [P, 2, E], F32)
        x_res = m.sb("x_res", [P, 2, E], F32)
        assert m.at <= nc.sbuf_usable_end, m.at
        lora_raw = Map(lora_at).sb("lora_raw", [P, 2 * (E + H)], F32)
        m = Map(phase_at)
        q_int = m.sb("q_int", [P, 2, 2, E], I32)
        w_real = m.sb("w_real", [P, 2, 2, E], F32)
        up_w = [[m.sb(f"up_w{n}_{h}", [P, KT_E, P], F32R) for h in range(2)] for n in range(EARLY)]
        down_w = [[m.sb(f"down_w{n}_{h}", [P, E], F32R) for h in range(2)] for n in range(EARLY)]
        assert m.at <= rows_at
        m = Map(rows_at)
        zT = [m.sb(f"zT{h}", [P, KT_E, CHUNK], F32R) for h in range(2)]
        hid_raw = m.sb("hid_raw", [P, CHUNK], F32)
        hid_high = [m.sb("hid_high0", [P, CHUNK], F32R)]
        assert m.at <= rest_at - 4 * GB * E
        y_in = Map(rest_at - 4 * GB * E).sb("y_in", [P, CT, E], F32)
        m = Map(rest_at)
        hid_high.append(m.sb("hid_high1", [P, CHUNK], F32R))
        hid_low = [m.sb(f"hid_low{n}", [P, CHUNK], F32R) for n in range(2)]
        hidT = [hid_high, hid_low]
        for n in range(EARLY, HT):
            up_w.append([m.sb(f"up_w{n}_{h}", [P, KT_E, P], F32R) for h in range(2)])
            down_w.append([m.sb(f"down_w{n}_{h}", [P, E], F32R) for h in range(2)])
        assert m.at <= nc.sbuf_usable_end, m.at

        ps = ctx.enter_context(nc.psum_tensor("ps", [P, 8, 512], F32))
        QK, LN_T, V_NEW, SCORES, P_T, AV = 0, 2, 3, 4, 5, 6
        FIRST_T = (LN_T, V_NEW, SCORES, P_T)
        LORA_UP, LORA_DOWN, HID, ACC = 0, 1, 3, (5, 6, 7, 2)
        Z_FIRST, Z_LATER = (7, 2, 0, 1), (0, 1, HID, 1)

        def sem(name):
            return ctx.enter_context(nc.semaphore(name))

        s_x = [sem(f"s_x{n}") for n in range(GB)]
        s_xres = [sem(f"s_xres{n}") for n in range(2)]
        s_kctx = [sem(f"s_kctx{n}") for n in range(GB)]
        s_vctx = [sem(f"s_vctx{n}") for n in range(2)]
        s_mask = [sem(f"s_mask{n}") for n in range(2)]
        s_wk = [sem(f"s_wk{n}") for n in range(KT_E)]
        s_w = {n: sem(f"s_w{n}") for n in (0, 2)}
        s_bias = sem("s_bias")
        s_lora_in = sem("s_lora_in")
        s_ymid = [sem(f"s_ymid{n}") for n in range(2)]
        s_y = [sem(f"s_y{n}") for n in range(CT)]
        s_res = [sem(f"s_res{n}") for n in range(CT)]
        s_q = [sem(f"s_q{n}") for n in range(2)]
        s_out = [sem(f"s_out{n}") for n in range(CT)]
        xt_t = sem("xt_t")
        kproj = sem("kproj")
        qproj = sem("qproj")
        vproj = sem("vproj")
        scored = sem("scored")
        p_t = sem("p_t")
        av_done = sem("av_done")
        z_t = sem("z_t")
        lora_up_done = sem("lora_up_done")
        lora_down_done = sem("lora_down_done")
        up_done = sem("up_done")
        down_done = sem("down_done")
        wk_hi = sem("wk_hi")
        w_hi = sem("w_hi")
        lora_hi = sem("lora_hi")
        xt_evac = sem("xt_evac")
        xt_hi = sem("xt_hi")
        k_evac = sem("k_evac")
        q_hi = sem("q_hi")
        k_hi = sem("k_hi")
        v_hi = sem("v_hi")
        exp_done = sem("exp_done")
        p_hi = sem("p_hi")
        z_hi = sem("z_hi")
        up_hi = sem("up_hi")
        down_hi = sem("down_hi")
        hid_hi = sem("hid_hi")
        wk_lo = sem("wk_lo")
        w_lo = sem("w_lo")
        lora_lo = sem("lora_lo")
        lora_lo_v = sem("lora_lo_v")
        bq_ready = sem("bq_ready")
        stats = sem("stats")
        stats_step = sem("stats_step")
        norm = sem("norm")
        xt_lo = sem("xt_lo")
        q_lo = sem("q_lo")
        k_lo = sem("k_lo")
        v_evac = sem("v_evac")
        v_lo = sem("v_lo")
        maxed = sem("maxed")
        soft = sem("soft")
        inv = sem("inv")
        p_lo = sem("p_lo")
        y_done = sem("y_done")
        z_lo = sem("z_lo")
        scaled = sem("scaled")
        up_real = sem("up_real")
        down_real = sem("down_real")
        up_lo = sem("up_lo")
        down_lo = sem("down_lo")
        hid_lo = sem("hid_lo")
        out_done = sem("out_done")
        const_step = sem("const_step")
        const_ready = sem("const_ready")
        pads = sem("pads")
        lora_zero = sem("lora_zero")
        root = sem("root")
        res_ready = sem("res_ready")

        block = ctx.enter_context(nc.Block())

        LAST = GROUPS - 1

        def groups(eng, body):
            body(0, True, False)
            with eng.Fori(1, LAST) as g:
                body(g, False, False)
            body(LAST, False, True)

        def chunks(eng, body):
            body(0, CT, CT, True)
            with eng.Fori(1, FULL - 1) as c:
                body(c, CT, CT, False)
            body(FULL - 1, CT, REST, False)
            body(FULL, REST, 0, False)

        UP_A, UP_B, DOWN_A, DOWN_B = 0, E, E + H, E + 2 * H
        LORA_LOWS = ((0, UP_A, slice(64, 128), E), (0, UP_B, slice(32, 64), H), (0, UP_B, slice(96, 128), H),
                     (1, DOWN_B, slice(32, 64), E), (1, DOWN_B, slice(96, 128), E))
        LORA_LOW_V = (1, DOWN_A, slice(64, 128), H)


        @block.sync
        def _(sp):
            def load_x(b, slot):
                sp.dma_start(x_in[0:S, slot, :], x[b]).then_inc(s_x[slot], 16)

            def load_mask(b, slot):
                sp.dma_start(mask_sb[0:S, slot, 0:KEYS], mask[b]).then_inc(s_mask[slot], 16)

            def load_k(b, i):
                sp.dma_start(k_raw[:, i, :, S:KEYS], ctx_k[b]).then_inc(s_kctx[i], 16)

            def load_v(b, slot):
                sp.dma_start(v_raw[S:P, slot, 0, :], ctx_v[b, 0:P - S, :]).then_inc(s_vctx[slot], 16)
                sp.dma_start(v_raw[:, slot, 1:3, :],
                             ctx_v[b, P - S:VROWS, :].rearrange("(t p) e -> p t e", p=P)).then_inc(s_vctx[slot], 16)

            def load_res(b, slot):
                sp.dma_start(x_res[0:S, slot, :], x[b]).then_inc(s_xres[slot], 16)

            load_x(0, 0)
            for k in range(KT_E):
                cols = slice(k * E, (k + 1) * E)
                sp.dma_start(w_stage[:, 1, cols], w_qkv[1, :, cols]).then_inc(s_wk[k], 16)
                if k == 0:
                    for b in range(1, GB):
                        load_x(b, b)
            sp.dma_start(bqk_col[:], b_qk).then_inc(s_bias, 16)
            sp.dma_start(w_stage[:, 0, :], w_qkv[0]).then_inc(s_w[0], 16)
            sp.dma_start(bup_col[:], b_up).then_inc(s_bias, 16)
            sp.dma_start(bv_row[:], b_v.partition_broadcast(P)).then_inc(s_bias, 16)
            sp.dma_start(bdown_row[:], b_down.partition_broadcast(P)).then_inc(s_bias, 16)
            sp.dma_start(w_stage[:, 2, :], w_qkv[2]).then_inc(s_w[2], 16)
            for i in range(GB):
                sp.wait_ge(norm, i + 1)
                load_x(GB + i, i)
            load_k(0, 0)
            sp.wait_ge(lora_zero, 1)
            for quadrant in range(4):
                sp.dma_start(lora_raw[quadrant * 32:quadrant * 32 + R, :], lora).then_inc(s_lora_in, 16)
            load_mask(0, 0)
            for i in range(1, GB):
                load_k(i, i)
            load_v(0, 0)
            sp.wait_ge(lora_lo_v, 1)
            sp.wait_ge(lora_lo, len(LORA_LOWS))
            load_v(1, 1)

            def group(g, first, last):
                for i in range(0 if first else GB):
                    if not last:
                        sp.wait_ge(norm, g * GB + i + 1)
                        load_x(g * GB + GB + i, i)
                    else:
                        if i == 0:
                            sp.wait_ge(s_ymid[0], 16 * ((CHUNK - 1) // S // 2 + 1))
                            sp.wait_ge(s_ymid[1], 16 * (((CHUNK - 1) // S + 1) // 2))
                            sp.wait_ge(norm, B)
                        load_y(i, i)
                for i in range(GB):
                    b = g * GB + i
                    if not (first and i < 2):
                        sp.wait_ge(y_done, b - 1)
                    load_res(b, i % 2)
                    if not (first and i < 2):
                        sp.wait_ge(v_lo, b - 1)
                        load_v(b, i % 2)
                    if not (last and i == GB - 1):
                        if not (first and i == 0):
                            sp.wait_ge(maxed, b)
                        load_mask(b + 1, (i + 1) % 2)
                    if not (first and i == 0) and not (last and i > 0):
                        sp.wait_ge(k_lo, b)
                        load_k(b + GB - 1, (i - 1) % GB)
                    if last and i < EARLY:
                        if i == 0:
                            sp.wait_ge(qproj, GROUPS * KT_E)
                        load_w(i)

            def load_y(t, slot):
                sp.dma_start(y_in[:, slot, :], y_mid_rows[bass.ts(t, P), :]).then_inc(s_y[slot], 16)

            def load_w(n):
                k = n % 2
                sp.dma_start(q_int[:, k, 0, :], up_q[n]).then_inc(s_q[k], 16)
                sp.dma_start(q_int[:, k, 1, :], down_q[n]).then_inc(s_q[k], 16)
                for half in range(2):
                    rows = slice(half * (P // 2), (half + 1) * (P // 2))
                    for part, scales in enumerate((up_s, down_s)):
                        sp.dma_start(w_real[rows, k, part, :],
                                     scales[half, n].partition_broadcast(P // 2)).then_inc(s_q[k], 16)

            groups(sp, group)

            def next_rows(c, following):
                for j in range(following):
                    sp.wait_ge(z_t, c * CT + j + 1)
                    load_y(c * CT + CT + j, j)

            for n in range(EARLY, HT):
                if n == 6:
                    for k in range(2):
                        sp.wait_ge(s_ymid[k], 16 * (B // 2))
                    next_rows(0, CT)
                sp.wait_ge(up_lo, n - 1)
                sp.wait_ge(down_lo, n - 1)
                load_w(n)

            def chunk(c, tiles, following, first):
                if first:
                    sp.wait_ge(lora_up_done, HT)
                    sp.wait_ge(lora_down_done, HT)
                else:
                    next_rows(c, following)
                for j in range(tiles):
                    if not first:
                        sp.wait_ge(s_out[j], 16 * c)
                    sp.dma_start(y_res[:, j, :], y_mid_rows[bass.ts(c * CT + j, P), :]).then_inc(s_res[j], 16)

            chunks(sp, chunk)
            for j in range(CT):
                sp.wait_ge(s_out[j], 16 * (FULL + (j < REST)))

        @block.gpsimd
        def _(pool):
            pool.memset(ident[:], 0.0).then_inc(const_step, 1)
            pool.memset(minus_half[:], -0.5).then_inc(const_step, 1)
            pool.wait_ge(const_step, 2)
            pool.affine_select(out=ident[:], in_=ident[:], compare_op=ALU.not_equal, fill=1.0, base=0,
                               pattern=[[-1, P]], channel_multiplier=1).then_inc(const_ready, 1)
            pool.memset(lora_raw[:], 0.0).then_inc(lora_zero, 1)
            pool.memset(k_raw[:, :, :, KEYS:KPAD], 0.0).then_inc(pads, 1)
            pool.memset(probs[:, :, KEYS:3 * P], 0.0).then_inc(pads, 1)

            def inv_root(n, slot, rows):
                pool.wait_ge(stats, n + 1)
                pool.tensor_tensor(rstd[0:rows, slot, :], var_eps[0:rows, slot, :], minus_half[0:rows, :],
                                   ALU.pow).then_inc(root, 1)

            for b in range(GB):
                inv_root(b, b, S)

            def store_mid(b, slot):
                pool.wait_ge(y_done, b + 1)
                pool.dma_start(y_mid[b], y_out[0:S, slot, :]).then_inc(s_ymid[slot], 16)

            def lora_low(which):
                half, at, rows, n = LORA_LOWS[which]
                pool.wait_ge(lora_hi, half + 1)
                if which == 0:
                    pool.wait_ge(root, GB + 2)
                elif which == 1:
                    pool.wait_ge(root, 2 * GB)
                else:
                    pool.wait_ge(lora_lo, which)
                part = lora_w[rows, at:at + n]
                pool.tensor_tensor(part, lora_raw[rows, at:at + n], part.bitcast(F32),
                                   ALU.subtract).then_inc(lora_lo, 1)

            def group(g, first, last):
                if not first:
                    store_mid(g * GB - 2, 0)
                for i in range(GB):
                    inv_root(g * GB + GB + i, i, P if last else S)
                    if first and i == 1:
                        lora_low(0)
                        pool.wait_ge(lora_lo, 1)
                if first:
                    for which in range(1, len(LORA_LOWS)):
                        lora_low(which)
                    pool.wait_ge(lora_lo, len(LORA_LOWS))
                if not first:
                    store_mid(g * GB - 1, 1)
                for i in range(GB - 2):
                    store_mid(g * GB + i, i % 2)

            groups(pool, group)
            store_mid(B - 2, 0)
            store_mid(B - 1, 1)

            def chunk(c, tiles, following, first):
                for j in range(following):
                    inv_root(c * CT + (B + CT + j), j, P)
                for j in range(tiles):
                    pool.wait_ge(s_res[j], 16 * c + 16)
                    pool.tensor_tensor(y_res[:, j, :], y_res[:, j, :], bdown_row[:], ALU.add).then_inc(res_ready, 1)
                for j in range(tiles):
                    pool.wait_ge(out_done, c * CT + j + 1)
                    pool.dma_start(out[bass.ts(c * CT + j, P), :], y_res[:, j, :]).then_inc(s_out[j], 16)

            chunks(pool, chunk)

        @block.scalar
        def _(act):
            def w_high(which):
                act.wait_ge(s_w[which], 16)
                high = wv_split[0][:] if which == 2 else qk_split[0][:, which, :, :]
                act.activation(high.rearrange("p k f -> p (k f)"), w_stage[:, which, :],
                               ACT.Copy, scale=SCALE if which == 0 else 1.0).then_inc(w_hi, 1)

            def xt_evacuate(b, i):
                act.wait_ge(xt_t, b + 1)
                act.activation(xT_next[:, :, i * S:(i + 1) * S],
                               ps[:, LN_T, 0:KT_E * S].rearrange("p (k s) -> p k s", k=KT_E),
                               ACT.Copy).then_inc(xt_evac, 1)

            def v_high(b, half_b, slot):
                act.wait_ge(v_evac, b + 1)
                act.wait_ge(s_vctx[slot], half_b * 32 + 32)
                act.wait_ge(av_done, b)
                act.activation(v_split[0][:], v_raw[:, slot, :, :], ACT.Copy).then_inc(v_hi, 1)

            def v_high_first():
                act.wait_ge(v_evac, 1)
                act.wait_ge(s_vctx[0], 32)
                act.wait_ge(lora_lo_v, 1)
                act.wait_ge(lora_lo, len(LORA_LOWS))
                act.activation(v_split[0][:], v_raw[:, 0, :, :], ACT.Copy).then_inc(v_hi, 1)

            def p_high(b, first):
                act.wait_ge(p_t, b + 1)
                if not first:
                    act.wait_ge(av_done, b)
                act.activation(pT[0][:].rearrange("p t s -> p (t s)"), ps[:, P_T, 0:3 * S],
                               ACT.Copy).then_inc(p_hi, 1)

            def k_high(g, i, first):
                b = g * GB + i
                act.wait_ge(k_evac, g * KT_E + KT_E)
                act.wait_ge(s_kctx[i], 16 * g + 16)
                if first and i == 0:
                    act.wait_ge(pads, 2)
                else:
                    act.wait_ge(scored, b)
                act.activation(kT[0][:], k_raw[:, i, :, :], ACT.Copy).then_inc(k_hi, 1)

            def wk_high(k):
                act.wait_ge(s_wk[k], 16)
                act.activation(qk_split[0][:, 1, k, :], w_stage[:, 1, k * E:(k + 1) * E], ACT.Copy).then_inc(wk_hi, 1)

            wk_high(0)
            wk_high(1)
            for i in range(GB):
                act.wait_ge(xt_t, i + 1)
                act.activation(xT[0][:, :, i * S:(i + 1) * S],
                               ps[:, FIRST_T[i], 0:KT_E * S].rearrange("p (k s) -> p k s", k=KT_E),
                               ACT.Copy).then_inc(xt_hi, 1)
                if i == 1:
                    wk_high(2)
                    wk_high(3)

            def group(g, first, last):
                for k in range(0 if first else KT_E):
                    if k == 0:
                        act.wait_ge(xt_evac, g * GB)
                        act.wait_ge(vproj, g * GB)
                    act.activation(xT[0][:, k, :], xT_next[:, k, :], ACT.Copy).then_inc(xt_hi, 1)
                if not first:
                    v_high(g * GB - 1, g * 2 - 1, 1)
                    p_high(g * GB - 1, False)
                for f in range(KT_E):
                    if first and f < 2:
                        w_high(2 * f)
                    if first and f == 0:
                        act.wait_ge(s_bias, 64)
                    act.wait_ge(kproj, g * KT_E + f + 1)
                    if not first:
                        act.wait_ge(k_lo, g * GB)
                    act.activation(k_raw[:, :, f, 0:S],
                                   ps[:, QK + f % 2, 0:GS].rearrange("p (b s) -> p b s", b=GB),
                                   ACT.Identity, bias=bqk_col[:, KT_E + f:KT_E + f + 1]).then_inc(k_evac, 1)
                k_high(g, 0, first)
                if first:
                    act.wait_ge(bq_ready, 1)
                for f in range(KT_E):
                    act.wait_ge(qproj, g * KT_E + f + 1)
                    act.activation(qT[0][:, f, :], ps[:, QK + f % 2, 0:GS], ACT.Identity,
                                   bias=bq_scaled[:, f:f + 1]).then_inc(q_hi, 1)
                    if not last:
                        if f == 0 and not first:
                            act.wait_ge(xt_lo, g * KT_E + KT_E)
                        xt_evacuate(g * GB + GB + f, f)
                for i in range(GB):
                    b = g * GB + i
                    if i == 1 and first:
                        v_high_first()
                        p_high(0, True)
                    elif i > 0:
                        v_high(b - 1, g * 2 + (i - 1) // 2, (i - 1) % 2)
                        p_high(b - 1, False)
                    if i < GB - 1:
                        k_high(g, i + 1, first)
                    act.wait_ge(soft, b + 1)
                    if not (first and i < 2):
                        act.wait_ge(p_t, b - 1)
                        act.wait_ge(inv, b - 1)
                    act.activation(probs[0:S, i % 2, 0:KEYS], logits[0:S, i % 2, 0:KEYS], ACT.Exp,
                                   bias=minus_max[0:S, i % 2, :],
                                   accum_out=row_sum[0:S, i % 2, :]).then_inc(exp_done, 1)
                    if last and i == GB - 1:
                        for j in range(CT):
                            z_high(j, j, Z_FIRST)
                    if last and i >= 2:
                        up_high(i - 2)
                        down_high(i - 2)

            def z_high(t, j, banks):
                act.wait_ge(z_t, t + 1)
                act.activation(zT[0][:, :, j * P:(j + 1) * P],
                               ps[:, banks[j], :].rearrange("p (k s) -> p k s", k=KT_E),
                               ACT.Copy).then_inc(z_hi, 1)

            def hidden(c, n, width, first):
                act.wait_ge(up_done, c * HT + n + 1)
                if not (first and n == 0):
                    act.wait_ge(hid_lo, c * HT + n)
                act.activation(hid_raw[:, 0:width], ps[:, HID + n % 2, 0:width], ACT.Relu,
                               bias=bup_col[:, n:n + 1])
                if not (first and n < 2):
                    act.wait_ge(down_done, c * HT + n - 1)
                act.activation(hidT[0][n % 2][:, 0:width], ps[:, HID + n % 2, 0:width], ACT.Relu,
                               bias=bup_col[:, n:n + 1]).then_inc(hid_hi, 1)

            def up_high(n):
                act.wait_ge(up_real, n + 1)
                act.activation(up_w[n][0][:].rearrange("p k h -> p (k h)"), w_real[:, n % 2, 0, :],
                               ACT.Copy).then_inc(up_hi, 1)

            def down_high(n):
                act.wait_ge(down_real, n + 1)
                act.activation(down_w[n][0][:], w_real[:, n % 2, 1, :], ACT.Copy).then_inc(down_hi, 1)

            groups(act, group)
            p_high(B - 1, False)
            v_high(B - 1, B // 2 - 1, 1)

            def chunk(c, tiles, following, first):
                for n in range(HT):
                    if first and n + EARLY < HT:
                        if n == 1:
                            act.wait_ge(y_done, B)
                            for k in range(2):
                                act.wait_ge(s_ymid[k], 16 * (B // 2))
                        up_high(n + EARLY)
                    hidden(c, n, tiles * P, first)
                    if first and n + EARLY < HT:
                        down_high(n + EARLY)
                for j in range(following):
                    if j == 0:
                        act.wait_ge(up_done, c * HT + HT)
                    z_high(c * CT + CT + j, j, Z_LATER)

            chunks(act, chunk)

        @block.vector
        def _(dve):
            def ln_stats(n, src, slot, rows):
                dve.bn_stats(bn_raw[0:rows, slot, :], src).then_inc(stats_step, 1)
                dve.wait_ge(stats_step, 2 * n + 1)
                dve.memset(gate[:], 0.0)
                dve.bn_aggr(mean_var[0:rows, slot, :], bn_raw[0:rows, slot, :]).then_inc(stats_step, 1)
                dve.wait_ge(stats_step, 2 * n + 2)
                dve.tensor_scalar(var_eps[0:rows, slot, :], mean_var[0:rows, slot, 1:2], EPS, None,
                                  ALU.add).then_inc(stats, 1)

            def ln_apply(n, dst, src, slot, rows):
                dve.wait_ge(root, n + 1)
                dve.tensor_scalar(dst, src, mean_var[0:rows, slot, 0:1], rstd[0:rows, slot, :],
                                  ALU.subtract, ALU.mult).then_inc(norm, 1)

            def x_stats(g, i):
                dve.wait_ge(s_x[i], g * 16 + 16)
                ln_stats(g * GB + i, x_in[0:S, i, :], i, S)

            def x_apply(b, i, fresh):
                if not fresh:
                    dve.wait_ge(xt_t, b - 1)
                ln_apply(b, x_norm[0:S, i % 2, :], x_in[0:S, i, :], i, S)

            def w_low(which, n):
                dve.wait_ge(w_hi, n + 1)
                hi, lo = ((wv_split[h][:] if which == 2 else qk_split[h][:, which, :, :]).rearrange("p k f -> p (k f)")
                          for h in range(2))
                hi = hi.bitcast(F32)
                dve.scalar_tensor_tensor(lo, w_stage[:, which, :], SCALE if which == 0 else 1.0, hi,
                                         ALU.mult, ALU.subtract).then_inc(w_lo, 1)

            def wk_low(k):
                dve.wait_ge(wk_hi, k + 1)
                dve.tensor_tensor(qk_split[1][:, 1, k, :], w_stage[:, 1, k * E:(k + 1) * E],
                                  qk_split[0][:, 1, k, :].bitcast(F32), ALU.subtract).then_inc(wk_lo, 1)

            def xt_first_low(i):
                dve.wait_ge(xt_hi, i + 1)
                part = slice(i * S, (i + 1) * S)
                dve.tensor_tensor(xT[1][:, :, part],
                                  ps[:, FIRST_T[i], 0:KT_E * S].rearrange("p (k s) -> p k s", k=KT_E),
                                  xT[0][:, :, part].bitcast(F32), ALU.subtract).then_inc(xt_lo, 1)

            x_stats(0, 0)
            x_stats(0, 1)
            x_stats(0, 2)
            x_apply(0, 0, True)
            x_stats(0, 3)
            for b in range(1, GB):
                x_apply(b, b, b < 2)
            xt_first_low(0)
            xt_first_low(1)
            wk_low(0)
            xt_first_low(2)
            xt_first_low(3)
            for k in range(1, KT_E):
                wk_low(k)

            def v_evacuate(b, slot, fresh):
                dve.wait_ge(vproj, b + 1)
                if not fresh:
                    dve.wait_ge(v_lo, b - 1)
                elif slot == 1:
                    dve.wait_ge(lora_lo_v, 1)
                    dve.wait_ge(lora_lo, len(LORA_LOWS))
                dve.tensor_tensor(v_raw[0:S, slot, 0, :], ps[0:S, V_NEW, :], bv_row[0:S, :],
                                  ALU.add).then_inc(v_evac, 1)

            def v_low(b, slot):
                dve.wait_ge(v_hi, b + 1)
                dve.tensor_tensor(v_split[1][:], v_raw[:, slot, :, :], v_split[0][:].bitcast(F32),
                                  ALU.subtract).then_inc(v_lo, 1)

            def p_low(b):
                dve.wait_ge(p_hi, b + 1)
                dve.tensor_tensor(pT[1][:].rearrange("p t s -> p (t s)"), ps[:, P_T, 0:3 * S],
                                  pT[0][:].rearrange("p t s -> p (t s)").bitcast(F32),
                                  ALU.subtract).then_inc(p_lo, 1)

            def k_low(b, i):
                dve.wait_ge(k_hi, b + 1)
                dve.tensor_tensor(kT[1][:], k_raw[:, i, :, :], kT[0][:].bitcast(F32),
                                  ALU.subtract).then_inc(k_lo, 1)

            def softmax_shift(b, half_b, slot, fresh):
                dve.wait_ge(scored, b + 1)
                dve.wait_ge(s_mask[slot], half_b * 16 + 16)
                if not fresh:
                    dve.wait_ge(exp_done, b - 1)
                dve.memset(gate[:], 0.0)
                dve.tensor_tensor_reduce(logits[0:S, slot, 0:KEYS], ps[0:S, SCORES, 0:KEYS],
                                         mask_sb[0:S, slot, 0:KEYS], 1.0, -3.0e38, ALU.add, ALU.max,
                                         row_max[0:S, slot, :]).then_inc(maxed, 1)
                dve.wait_ge(maxed, b + 1)
                dve.tensor_scalar(minus_max[0:S, slot, :], row_max[0:S, slot, :], -1.0, None,
                                  ALU.mult).then_inc(soft, 1)

            def attended(b, half_b, slot, fresh):
                dve.wait_ge(exp_done, b + 1)
                dve.reciprocal(inv_sum[0:S, slot, :], row_sum[0:S, slot, :]).then_inc(inv, 1)
                dve.wait_ge(inv, b + 1)
                dve.wait_ge(av_done, b + 1)
                dve.wait_ge(s_xres[slot], half_b * 16 + 16)
                if not fresh:
                    dve.wait_ge(s_ymid[slot], half_b * 16)
                dve.scalar_tensor_tensor(y_out[0:S, slot, :], ps[0:S, AV, :], inv_sum[0:S, slot, :],
                                         x_res[0:S, slot, :], ALU.mult, ALU.add).then_inc(y_done, 1)

            def lora_high(half):
                dve.wait_ge(s_lora_in, 64)
                if half == 0:
                    dve.wait_ge(wk_lo, KT_E)
                    dve.wait_ge(w_lo, 2)
                cols = slice(half * (E + H), (half + 1) * (E + H))
                dve.tensor_copy(lora_w[:, cols], lora_raw[:, cols]).then_inc(lora_hi, 1)

            def rows_stats(g, i, last):
                if last:
                    y_stats(i, 16, i)
                else:
                    x_stats(g + 1, i)

            def rows_apply(g, i, last):
                if last:
                    y_apply(i, i)
                else:
                    x_apply(g * GB + GB + i, i, False)

            def group(g, first, last):
                for k in range(0 if first else KT_E):
                    dve.wait_ge(xt_hi, g * KT_E + k + 1)
                    dve.tensor_tensor(xT[1][:, k, :], xT_next[:, k, :], xT[0][:, k, :].bitcast(F32),
                                      ALU.subtract).then_inc(xt_lo, 1)
                if first:
                    w_low(0, 0)
                    w_low(2, 1)
                    dve.wait_ge(s_bias, 64)
                    dve.tensor_scalar(bq_scaled[:], bqk_col[:, 0:KT_E], SCALE, None, ALU.mult).then_inc(bq_ready, 1)
                    lora_high(0)
                else:
                    attended(g * GB - 2, g * 2 - 1, 0, False)
                    v_low(g * GB - 1, 1)
                    p_low(g * GB - 1)
                rows_stats(g, 0, last)
                rows_stats(g, 1, last)
                rows_apply(g, 0, last)
                rows_apply(g, 1, last)
                if first:
                    lora_high(1)
                rows_stats(g, 2, last)
                rows_stats(g, 3, last)
                for f in range(KT_E):
                    dve.wait_ge(q_hi, g * KT_E + f + 1)
                    dve.scalar_tensor_tensor(qT[1][:, f, :], ps[:, QK + f % 2, 0:GS], bq_scaled[:, f:f + 1],
                                             qT[0][:, f, :].bitcast(F32), ALU.add, ALU.subtract).then_inc(q_lo, 1)
                    if f < 2:
                        rows_apply(g, 2 + f, last)
                    elif f == 2:
                        k_low(g * GB, 0)
                if first:
                    _, at, rows, n = LORA_LOW_V
                    part = lora_w[rows, at:at + n]
                    dve.wait_ge(lora_hi, 2)
                    dve.tensor_tensor(part, lora_raw[rows, at:at + n], part.bitcast(F32),
                                      ALU.subtract).then_inc(lora_lo_v, 1)
                else:
                    attended(g * GB - 1, g * 2 - 1, 1, False)
                for i in range(GB):
                    b = g * GB + i
                    if i > 0:
                        v_low(b - 1, (i - 1) % 2)
                        p_low(b - 1)
                    softmax_shift(b, g * 2 + i // 2, i % 2, first and i < 2)
                    if i < GB - 1:
                        k_low(b + 1, i + 1)
                    v_evacuate(b, i % 2, first and i < 2)
                    if 0 < i < GB - 1:
                        attended(b - 1, g * 2, i - 1, first)
                    if last and i == GB - 1:
                        for j in range(CT):
                            z_low(j, j, Z_FIRST)
                    if last and i >= 2:
                        weights_low(i - 2)
                    if last and 1 <= i <= EARLY:
                        add_products(i - 1)
                    if last and i < EARLY:
                        dequantise(i)

            def y_stats(t, c16, j):
                dve.wait_ge(s_y[j], c16)
                ln_stats(t + B, y_in[:, j, :], j, P)

            def y_apply(t, j):
                ln_apply(t + B, y_in[:, j, :], y_in[:, j, :], j, P)

            def z_low(t, j, banks):
                dve.wait_ge(z_hi, t + 1)
                dve.tensor_tensor(zT[1][:, :, j * P:(j + 1) * P],
                                  ps[:, banks[j], :].rearrange("p (k s) -> p k s", k=KT_E),
                                  zT[0][:, :, j * P:(j + 1) * P].bitcast(F32), ALU.subtract).then_inc(z_lo, 1)

            def dequantise(n):
                k = n % 2
                dve.wait_ge(s_q[k], 96 * (n // 2) + 96)
                for part in range(2):
                    w = w_real[:, k, part, :]
                    dve.scalar_tensor_tensor(w, q_int[:, k, part, :], -ZERO_POINT, w,
                                             ALU.add, ALU.mult).then_inc(scaled, 1)

            def add_products(n):
                for part, bank, real, product in ((0, LORA_UP, up_real, lora_up_done),
                                                  (1, LORA_DOWN, down_real, lora_down_done)):
                    w = w_real[:, n % 2, part, :]
                    dve.wait_ge(scaled, 2 * n + part + 1)
                    dve.wait_ge(product, n + 1)
                    dve.tensor_tensor(w, ps[:, bank, :], w, ALU.add).then_inc(real, 1)

            def weights_low(n):
                k = n % 2
                dve.wait_ge(up_hi, n + 1)
                dve.tensor_tensor(up_w[n][1][:].rearrange("p k h -> p (k h)"), w_real[:, k, 0, :],
                                  up_w[n][0][:].rearrange("p k h -> p (k h)").bitcast(F32),
                                  ALU.subtract).then_inc(up_lo, 1)
                dve.wait_ge(down_hi, n + 1)
                dve.tensor_tensor(down_w[n][1][:], w_real[:, k, 1, :], down_w[n][0][:].bitcast(F32),
                                  ALU.subtract).then_inc(down_lo, 1)

            groups(dve, group)
            attended(B - 2, B // 2 - 1, 0, False)
            p_low(B - 1)
            v_low(B - 1, 1)

            def chunk(c, tiles, following, first):
                for n in range(HT):
                    if first and n + EARLY < HT:
                        dequantise(n + EARLY)
                        add_products(n + EARLY)
                        weights_low(n + EARLY)
                    if first and n == 0:
                        attended(B - 1, B // 2 - 1, 1, False)
                    if n % 2 == 0 and n >= HT // 2 and (n - HT // 2) // 2 < following:
                        j = (n - HT // 2) // 2
                        y_stats(c * CT + (CT + j), 16 * c + 32, j)
                    dve.wait_ge(hid_hi, c * HT + n + 1)
                    if not (first and n < 2):
                        dve.wait_ge(down_done, c * HT + n - 1)
                    dve.tensor_tensor(hidT[1][n % 2][:, 0:tiles * P], hid_raw[:, 0:tiles * P],
                                      hidT[0][n % 2][:, 0:tiles * P].bitcast(F32), ALU.subtract).then_inc(hid_lo, 1)
                    if n % 2 == 0 and n >= HT // 2 and (n - HT // 2) // 2 < following:
                        j = (n - HT // 2) // 2
                        y_apply(c * CT + (CT + j), j)
                for j in range(following):
                    z_low(c * CT + (CT + j), j, Z_LATER)
                for j in range(tiles):
                    dve.wait_ge(down_done, c * HT + HT)
                    dve.wait_ge(res_ready, c * CT + j + 1)
                    dve.tensor_tensor(y_res[:, j, :], ps[:, ACC[j], :], y_res[:, j, :], ALU.add).then_inc(out_done, 1)

            chunks(dve, chunk)

        @block.tensor
        def _(pe):
            def product(dst, lhs, rhs, steps, done=None):
                n = len(PASSES) * steps
                for s in range(steps):
                    for a, b in PASSES:
                        i = s * len(PASSES) + PASSES.index((a, b))
                        last = pe.matmul(dst, lhs(a, s), rhs(b, s), start=(i == 0), stop=(i == n - 1))
                if done is not None:
                    last.then_inc(done, 1)

            def x_transpose(b, slot, bank, fresh):
                pe.wait_ge(norm, b + 1)
                if not fresh:
                    pe.wait_ge(xt_evac, b - GB)
                for k in range(KT_E):
                    last = pe.transpose(ps[:, bank, k * S:(k + 1) * S], x_norm[0:S, slot, k * P:(k + 1) * P],
                                        ident[0:S, 0:S])
                last.then_inc(xt_t, 1)

            def p_transpose(b, slot, fresh):
                pe.wait_ge(exp_done, b + 1)
                if fresh:
                    pe.wait_ge(pads, 2)
                else:
                    pe.wait_ge(p_lo, b)
                for t in range(3):
                    last = pe.transpose(ps[:, P_T, t * S:(t + 1) * S], probs[0:S, slot, t * P:(t + 1) * P],
                                        ident[0:S, 0:S])
                last.then_inc(p_t, 1)

            def attend(b, fresh):
                pe.wait_ge(p_lo, b + 1)
                pe.wait_ge(v_lo, b + 1)
                if not fresh:
                    pe.wait_ge(y_done, b)
                product(ps[0:S, AV, :], lambda h, t: pT[h][:, t, :], lambda h, t: v_split[h][:, t, :], 3, av_done)

            pe.wait_ge(const_ready, 1)
            for b in range(GB):
                x_transpose(b, b % 2, FIRST_T[b], True)

            def group(g, first, last):
                for which, done in ((1, kproj), (0, qproj)):
                    if first and which == 0:
                        pe.wait_ge(w_lo, 1)
                    for f in range(KT_E):
                        if which == 1 and f < 2 and not first:
                            pe.wait_ge(q_lo, g * KT_E - 1 + f)
                        elif which == 1 and f >= 2:
                            pe.wait_ge(k_evac, g * KT_E + f - 1)
                        elif which == 0 and f < 2:
                            pe.wait_ge(k_evac, g * KT_E + f + 3)
                        elif which == 0:
                            pe.wait_ge(q_lo, g * KT_E + f - 1)
                        for k in range(KT_E):
                            if which == 1 and f == 0 and first:
                                pe.wait_ge(xt_lo, GB)
                                pe.wait_ge(wk_lo, k + 1)
                            elif which == 1 and f == 0:
                                pe.wait_ge(xt_lo, g * KT_E + k + 1)
                            for a, b in PASSES:
                                mm = pe.matmul(ps[:, QK + f % 2, 0:GS],
                                               qk_split[a][:, which, k, f * P:(f + 1) * P], xT[b][:, k, :],
                                               start=(k == 0 and (a, b) == PASSES[0]),
                                               stop=(k == KT_E - 1 and (a, b) == PASSES[-1]))
                        mm.then_inc(done, 1)
                        if which == 0 and not last:
                            x_transpose(g * GB + GB + f, f % 2, LN_T, first and f == 0)
                if not first:
                    attend(g * GB - 1, False)
                for i in range(GB):
                    b = g * GB + i
                    pe.wait_ge(k_lo, b + 1)
                    pe.wait_ge(q_lo, g * KT_E + KT_E)
                    if not (first and i == 0):
                        pe.wait_ge(maxed, b)
                    product(ps[0:S, SCORES, 0:KPAD], lambda h, k: qT[h][:, k, i * S:(i + 1) * S],
                            lambda h, k: kT[h][:, k, :], KT_E, scored)
                    if first and i == 0:
                        pe.wait_ge(w_lo, 2)
                    else:
                        pe.wait_ge(v_evac, b)
                    product(ps[0:S, V_NEW, :], lambda h, k: xT[h][:, k, i * S:(i + 1) * S],
                            lambda h, k: wv_split[h][:, k, :], KT_E, vproj)
                    if last and i == 2:
                        lora_products(1)
                    if last and i == GB - 1:
                        pe.wait_ge(up_real, EARLY)
                        pe.wait_ge(down_real, EARLY)
                        for j in range(CT):
                            z_transpose(j, j, True, Z_FIRST)
                    if i > 0:
                        attend(b - 1, first and i == 1)
                    p_transpose(b, i % 2, first and i == 0)
                    if last and i == 0:
                        lora_products(0)

            def z_transpose(t, j, fresh, banks):
                pe.wait_ge(norm, t + B + 1)
                if not fresh:
                    pe.wait_ge(z_lo, t - 1)
                for k in range(KT_E):
                    last = pe.transpose(ps[:, banks[j], k * P:(k + 1) * P], y_in[:, j, k * P:(k + 1) * P], ident[:])
                last.then_inc(z_t, 1)

            def lora_products(n):
                pe.wait_ge(q_lo, GROUPS * KT_E)
                if n > 0:
                    pe.wait_ge(up_real, n)
                for k in range(KT_E):
                    last = pe.matmul(ps[:, LORA_UP, k * P:(k + 1) * P], lora_w[:, UP_A + k * P:UP_A + (k + 1) * P],
                                     lora_w[:, UP_B + n * P:UP_B + (n + 1) * P], start=True, stop=True)
                last.then_inc(lora_up_done, 1)
                if n > 0:
                    pe.wait_ge(down_real, n)
                pe.matmul(ps[:, LORA_DOWN, :], lora_w[:, DOWN_A + n * P:DOWN_A + (n + 1) * P],
                          lora_w[:, DOWN_B:DOWN_B + E], start=True, stop=True).then_inc(lora_down_done, 1)

            def up(c, n, width, first):
                if first:
                    pe.wait_ge(up_lo, n + 1)
                if not (first and n < 2):
                    pe.wait_ge(hid_hi, c * HT + n - 1)
                product(ps[:, HID + n % 2, 0:width], lambda h, k: up_w[n][h][:, k, :],
                        lambda h, k: zT[h][:, k, 0:width], KT_E, up_done)

            def down(c, n, tiles, first):
                if first:
                    pe.wait_ge(down_lo, n + 1)
                pe.wait_ge(hid_lo, c * HT + n + 1)
                for j in range(tiles):
                    if n == 0 and not first:
                        pe.wait_ge(out_done, (c - 1) * CT + j + 1)
                    for a, b in PASSES:
                        mm = pe.matmul(ps[:, ACC[j], :], hidT[a][n % 2][:, j * P:(j + 1) * P], down_w[n][b][:],
                                       start=(n == 0 and (a, b) == PASSES[0]),
                                       stop=(n == HT - 1 and (a, b) == PASSES[-1]))
                mm.then_inc(down_done, 1)

            groups(pe, group)

            def chunk(c, tiles, following, first):
                for n in range(HT):
                    if n == 0:
                        pe.wait_ge(z_lo, c * CT + tiles)
                    if first and n + EARLY < HT:
                        lora_products(n + EARLY)
                    if first and n == 0:
                        pe.wait_ge(v_evac, B)
                    if first and n == 1:
                        pe.wait_ge(maxed, B)
                    if n == HT - 1:
                        if first:
                            pe.wait_ge(up_real, HT)
                            pe.wait_ge(down_real, HT)
                        for j in range(min(2, following)):
                            z_transpose(c * CT + (CT + j), j, False, Z_LATER)
                    up(c, n, tiles * P, first)
                    if n == HT - 1 and following > 2:
                        pe.wait_ge(hid_hi, c * HT + HT - 1)
                        z_transpose(c * CT + (CT + 2), 2, True, Z_LATER)
                    if first and n == 0:
                        attend(B - 1, False)
                    if first and n == 1:
                        pe.wait_ge(y_done, B)
                    if n > 0:
                        down(c, n - 1, tiles, first)
                if following > 3:
                    z_transpose(c * CT + (CT + 3), 3, False, Z_LATER)
                down(c, HT - 1, tiles, first)

            chunks(pe, chunk)


def kernel(x, ctx_2048, mask_BxSxS2_ff0, L0_xattn_Wq, L0_xattn_bq, L0_xattn_Wk, L0_xattn_bk, L0_xattn_Wv,
           L0_xattn_bv, L0_ffn_w_up_q, L0_ffn_w_up_scale, L0_ffn_b_up, L0_ffn_w_up_lora_a, L0_ffn_w_up_lora_b,
           L0_ffn_w_down_q, L0_ffn_w_down_scale, L0_ffn_b_down, L0_ffn_w_down_lora_a, L0_ffn_w_down_lora_b):
    import concourse.bacc as bacc
    import numpy as np
    from concourse.bass_utils import run_bass_kernel_spmd

    x, ctx, mask = (np.asarray(a) for a in (x, ctx_2048, mask_BxSxS2_ff0))
    tail = ctx[:, :CTX]
    mask = np.concatenate([mask[:, :, CTX:], mask[:, :, :CTX]], axis=2)
    ctx_k = tail.reshape(B, CTX, KT_E, P).transpose(0, 3, 2, 1)
    ctx_v = np.zeros((B, VROWS, E), ctx.dtype)
    ctx_v[:, :CTX] = tail
    w_qkv = np.stack([np.asarray(w).reshape(E, KT_E, P).transpose(2, 1, 0).reshape(P, KT_E * E)
                      for w in (L0_xattn_Wq, L0_xattn_Wk, L0_xattn_Wv)])
    b_qk = np.concatenate([np.asarray(b).reshape(KT_E, P).T for b in (L0_xattn_bq, L0_xattn_bk)], axis=1)
    per = P // 64
    up_q = np.asarray(L0_ffn_w_up_q).reshape(HT, P, KT_E, P).transpose(0, 3, 2, 1).reshape(HT, P, E)
    up_s = np.asarray(L0_ffn_w_up_scale).reshape(HT, P, KT_E, per).transpose(3, 0, 2, 1).reshape(per, HT, E)
    down_q = np.asarray(L0_ffn_w_down_q).reshape(E, HT, P).transpose(1, 2, 0)
    down_s = np.asarray(L0_ffn_w_down_scale).reshape(E, HT, per).transpose(2, 1, 0)
    lora = np.concatenate([np.asarray(L0_ffn_w_up_lora_a).T, np.asarray(L0_ffn_w_up_lora_b),
                           np.asarray(L0_ffn_w_down_lora_a).T, np.asarray(L0_ffn_w_down_lora_b)], axis=1)
    arrays = {
        "x": x, "mask": mask, "ctx_k": ctx_k, "ctx_v": ctx_v, "w_qkv": w_qkv, "b_qk": b_qk,
        "b_v": np.asarray(L0_xattn_bv), "up_q": up_q, "up_s": up_s,
        "b_up": np.asarray(L0_ffn_b_up).reshape(HT, P).T, "down_q": down_q, "down_s": down_s,
        "b_down": np.asarray(L0_ffn_b_down), "lora": lora,
    }
    arrays = {f"in_{name}": np.ascontiguousarray(a) for name, a in arrays.items()}
    nc = bacc.Bacc("TRN2", target_bir_lowering=False, num_devices=1)
    args = {name[3:]: nc.dram_tensor(name, a.shape, mybir.dt.from_np(a.dtype), kind="ExternalInput").ap()
            for name, a in arrays.items()}
    y_mid = nc.dram_tensor("y_mid", (B, S, E), F32, kind="Internal").ap()
    out = nc.dram_tensor("out_0", (B * S, E), F32, kind="ExternalOutput").ap()
    build(nc, y_mid=y_mid, y_mid_rows=y_mid.rearrange("b s e -> (b s) e"), out=out, **args)
    result = run_bass_kernel_spmd(nc, [arrays], core_ids=[0])
    return result.results[0]["out_0"].reshape(B, S, E)
```
